# Optimizing a Trainium2 kernel written in Bass

```python
import numpy as np
import jax
import jax.numpy as jnp

def _softmax(x, axis=-1):
    return jax.nn.softmax(x, axis=axis)

def _gelu(x):
    return jax.nn.gelu(x, approximate=True)

def _silu(x):
    return jax.nn.silu(x)

def _sigmoid(x):
    return jax.nn.sigmoid(x)

def _layernorm(x, axis=-1, eps=1e-05):
    m = jnp.mean(x, axis=axis, keepdims=True)
    v = jnp.var(x, axis=axis, keepdims=True)
    return (x - m) / jnp.sqrt(v + eps)

def _scatter_add(tgt, idx, src, axis=0):
    return tgt.at[idx].add(src)

def _segment_sum(src, seg, n):
    return jax.ops.segment_sum(src, seg, n)
kernel_name = 'mk_xattn_ffn_d1_seqx_r2_0e7031'

def setup_inputs(seed: int=0):
    np.random.seed(seed)
    _w = jnp.asarray

    def _rec_inputs():
        import jax
        import jax.numpy as jnp
        _rk = jax.random.key(seed)
        x = 7.22e-05 + 1 * jax.random.normal(jax.random.fold_in(_rk, 1), (16, 256, 512), jnp.float32)
        _lenS = 256 - jax.random.randint(jax.random.fold_in(_rk, 7), (16,), 0, max(1, 256 // 4) + 1, jnp.int32)
        _lenS2 = 256 - jax.random.randint(jax.random.fold_in(_rk, 8), (16,), 0, max(1, 256 // 4) + 1, jnp.int32)
        _ctx_1024P = jax.random.normal(jax.random.fold_in(_rk, 11), (16, 16, 512), jnp.float32)
        _ctx_1024c = jax.random.dirichlet(jax.random.fold_in(_rk, 511), 0.3 * jnp.ones((16,), jnp.float32), (16, 256))
        _ctx_1024t = jnp.einsum('bsk,bkd->bsd', _ctx_1024c, _ctx_1024P)
        _ctx_1024t = _ctx_1024t * jax.lax.rsqrt(jnp.mean(jnp.square(_ctx_1024t)) + 1e-12) * 0.953939
        ctx_1024 = 4.13588e-05 + 0.999923 * (_ctx_1024t + 0.3 * jax.random.normal(jax.random.fold_in(_rk, 611), (16, 256, 512), jnp.float32))
        return (x, ctx_1024)
    x, ctx_1024 = _rec_inputs()

    def _L0_xattn_setup():
        import jax, jax.numpy as jnp
        import numpy as np
        import math
        DIM = 512
        HEADS = 16
        WINDOW = 128

        def _rope(x):
            b, s, d = x.shape
            half = d // 2
            inv_freq = 1.0 / 10000.0 ** (jnp.arange(half, dtype=jnp.float32) / half)
            ang = jnp.arange(s, dtype=jnp.float32)[:, None] * inv_freq[None, :]
            cos, sin = (jnp.cos(ang), jnp.sin(ang))
            x1, x2 = (x[..., :half], x[..., half:])
            return jnp.concatenate([x1 * cos - x2 * sin, x1 * sin + x2 * cos], axis=-1)
        key = jax.random.key(seed)
        ks = jax.random.split(key, 8)
        d = DIM
        q = jax.random.normal(ks[0], (2, 2048, d), dtype=jnp.float32)
        k = jax.random.normal(ks[1], (2, 2048, d), dtype=jnp.float32)
        v = jax.random.normal(ks[2], (2, 2048, d), dtype=jnp.float32)
        wq = jax.random.normal(ks[3], (d, d), dtype=jnp.float32) * 0.02
        wk = jax.random.normal(ks[4], (d, d), dtype=jnp.float32) * 0.02
        wv = jax.random.normal(ks[5], (d, d), dtype=jnp.float32) * 0.02
        wo_w = jax.random.normal(ks[6], (d, d), dtype=jnp.float32) * 0.02
        wo_b = jnp.zeros((d,), dtype=jnp.float32)
        return {'q': q, 'k': k, 'v': v, 'wq': wq, 'wk': wk, 'wv': wv, 'wo_w': wo_w, 'wo_b': wo_b}
    _L0_xattn_all = _L0_xattn_setup()
    _L0_xattn_in = {k: v for k, v in _L0_xattn_all.items() if k in ('wq', 'wk', 'wv', 'wo_w', 'wo_b')}
    del _L0_xattn_all

    def _L0_ffn_setup():
        import jax, jax.numpy as jnp
        import numpy as np

        def _ste(w, w_q):
            return w + jax.lax.stop_gradient(w_q - w)

        def quantize_w8_per(w, axis):
            amax = jnp.clip(jnp.max(jnp.abs(w), axis=axis, keepdims=True), 1e-08, None)
            scale = 127.0 / amax
            w_q = jnp.clip(jnp.round(w * scale), -128.0, 127.0) / scale
            return _ste(w, w_q)

        def quantize_a16(x):
            amax = jnp.clip(jnp.max(jnp.abs(x)), 1e-08, None)
            scale = 32767.0 / amax
            x_q = jnp.clip(jnp.round(x * scale), -32768.0, 32767.0) / scale
            return _ste(x, x_q)
        key = jax.random.key(seed)
        k1, k2, k3 = jax.random.split(key, 3)
        d_model, d_ff = (512, 2048)
        x = jax.random.normal(k1, (4, 1024, d_model), dtype=jnp.float32)
        W_in = jax.random.normal(k2, (d_model, d_ff), dtype=jnp.float32) / np.sqrt(d_model)
        b_in = jnp.zeros((d_ff,), dtype=jnp.float32)
        W_out = jax.random.normal(k3, (d_ff, d_model), dtype=jnp.float32) / np.sqrt(d_ff)
        b_out = jnp.zeros((d_model,), dtype=jnp.float32)
        return {'x': x, 'W_in': W_in, 'b_in': b_in, 'W_out': W_out, 'b_out': b_out}
    _L0_ffn_all = _L0_ffn_setup()
    _L0_ffn_in = {k: v for k, v in _L0_ffn_all.items() if k in ('W_in', 'b_in', 'W_out', 'b_out')}
    del _L0_ffn_all
    return {'x': x, 'ctx_1024': ctx_1024, 'L0_xattn_wq': _L0_xattn_in['wq'], 'L0_xattn_wk': _L0_xattn_in['wk'], 'L0_xattn_wv': _L0_xattn_in['wv'], 'L0_xattn_wo_w': _L0_xattn_in['wo_w'], 'L0_xattn_wo_b': _L0_xattn_in['wo_b'], 'L0_ffn_W_in': _L0_ffn_in['W_in'], 'L0_ffn_b_in': _L0_ffn_in['b_in'], 'L0_ffn_W_out': _L0_ffn_in['W_out'], 'L0_ffn_b_out': _L0_ffn_in['b_out']}

def reference(x, ctx_1024, L0_xattn_wq, L0_xattn_wk, L0_xattn_wv, L0_xattn_wo_w, L0_xattn_wo_b, L0_ffn_W_in, L0_ffn_b_in, L0_ffn_W_out, L0_ffn_b_out):
    import jax
    import jax.numpy as jnp

    def _L0_xattn_ref(q, k, v, wq, wk, wv, wo_w, wo_b):
        import jax, jax.numpy as jnp
        import numpy as np
        import math
        DIM = 512
        HEADS = 16
        WINDOW = 128

        def _rope(x):
            b, s, d = x.shape
            half = d // 2
            inv_freq = 1.0 / 10000.0 ** (jnp.arange(half, dtype=jnp.float32) / half)
            ang = jnp.arange(s, dtype=jnp.float32)[:, None] * inv_freq[None, :]
            cos, sin = (jnp.cos(ang), jnp.sin(ang))
            x1, x2 = (x[..., :half], x[..., half:])
            return jnp.concatenate([x1 * cos - x2 * sin, x1 * sin + x2 * cos], axis=-1)
        b, s, d = q.shape
        h, W = (HEADS, WINDOW)
        dk = d // h
        B = W
        nb = s // B
        qp = _rope(jnp.einsum('bsd,ed->bse', q, wq))
        kp = _rope(jnp.einsum('bsd,ed->bse', k, wk))
        vp = jnp.einsum('bsd,ed->bse', v, wv)
        qh = qp.reshape(b, s, h, dk).transpose(0, 2, 1, 3)
        kh = kp.reshape(b, s, h, dk).transpose(0, 2, 1, 3)
        vh = vp.reshape(b, s, h, dk).transpose(0, 2, 1, 3)
        kpad = jnp.pad(kh, ((0, 0), (0, 0), (B, B), (0, 0)))
        vpad = jnp.pad(vh, ((0, 0), (0, 0), (B, B), (0, 0)))
        kblk = kpad.reshape(b, h, nb + 2, B, dk)
        vblk = vpad.reshape(b, h, nb + 2, B, dk)
        kband = jnp.concatenate([kblk[:, :, i:i + nb] for i in range(3)], axis=3)
        vband = jnp.concatenate([vblk[:, :, i:i + nb] for i in range(3)], axis=3)
        qb = qh.reshape(b, h, nb, B, dk)
        scores = jnp.einsum('bhnqd,bhnkd->bhnqk', qb, kband) * math.sqrt(dk)
        n_idx = jnp.arange(nb)[:, None, None]
        qi = jnp.arange(B)[None, :, None]
        ki = jnp.arange(3 * B)[None, None, :]
        kpos = (n_idx - 1) * B + ki
        rel = ki - B - qi
        valid = (rel >= -W) & (rel <= W) & (kpos >= 0) & (kpos < s)
        neg = jnp.asarray(jnp.finfo(scores.dtype).min, scores.dtype)
        scores = jnp.where(valid[None, None], scores, neg)
        attn = jax.nn.softmax(scores, axis=-1)
        out = jnp.einsum('bhnqk,bhnkd->bhnqd', attn, vband)
        out = out.reshape(b, h, s, dk).transpose(0, 2, 1, 3).reshape(b, s, d)
        return jnp.einsum('bsd,ed->bse', out, wo_w) + wo_b

    def _L0_ffn_ref(x, W_in, b_in, W_out, b_out):
        import jax, jax.numpy as jnp
        import numpy as np

        def _ste(w, w_q):
            return w + jax.lax.stop_gradient(w_q - w)

        def quantize_w8_per(w, axis):
            amax = jnp.clip(jnp.max(jnp.abs(w), axis=axis, keepdims=True), 1e-08, None)
            scale = 127.0 / amax
            w_q = jnp.clip(jnp.round(w * scale), -128.0, 127.0) / scale
            return _ste(w, w_q)

        def quantize_a16(x):
            amax = jnp.clip(jnp.max(jnp.abs(x)), 1e-08, None)
            scale = 32767.0 / amax
            x_q = jnp.clip(jnp.round(x * scale), -32768.0, 32767.0) / scale
            return _ste(x, x_q)
        W_in_sim = quantize_w8_per(W_in, axis=0)
        W_out_sim = quantize_w8_per(W_out, axis=1)
        x_sim = quantize_a16(x)
        hidden = jax.nn.gelu(x_sim @ W_in_sim + b_in, approximate=False)
        hidden_sim = quantize_a16(hidden)
        out = hidden_sim @ W_out_sim + b_out
        return out
    x = x + _L0_xattn_ref(_layernorm(x, axis=-1), ctx_1024, ctx_1024, L0_xattn_wq, L0_xattn_wk, L0_xattn_wv, L0_xattn_wo_w, L0_xattn_wo_b)
    x = x + _L0_ffn_ref(_layernorm(x, axis=-1), L0_ffn_W_in, L0_ffn_b_in, L0_ffn_W_out, L0_ffn_b_out)
    return x

_drawn_inputs = setup_inputs


def setup_inputs(seed=0):
    import zlib

    import numpy as np

    out = dict(_drawn_inputs(seed))
    spreads = {'L0_xattn_wo_b': (0.0, 0.1), 'L0_ffn_b_in': (0.0, 0.1), 'L0_ffn_b_out': (0.0, 0.1)}
    factors = {}
    for name, (base, spread) in spreads.items():
        noise = np.random.default_rng([zlib.crc32(name.encode()), seed]).standard_normal(out[name].shape)
        drawn = base * np.exp(spread * noise) if base else spread * noise
        out[name] = jnp.asarray(drawn.astype(out[name].dtype))
    for name, factor in factors.items():
        out[name] = (out[name] * factor).astype(out[name].dtype)
    return out
```

```python
from contextlib import ExitStack

import numpy as np

import concourse.bass as bass
from concourse import mybir

ACT = mybir.ActivationFunctionType
ALU = mybir.AluOpType
AX_X = mybir.AxisListType.X
F32 = mybir.dt.float32
F32R = mybir.dt.float32r
BF16 = mybir.dt.bfloat16
F16 = mybir.dt.float16
I32 = mybir.dt.int32
ABSMAX = bass.bass_isa.ReduceOp.absmax

P = 128
NB, S, D = 16, 256, 512
H, DK = 16, 32
FF = 2048
TOK = NB * S
KC = D // P
NC4 = H // KC
WINDOW = 128
ROWT = P // DK
FC = FF // P
TT = 512
NT = TOK // TT
SUB = TT // P
KEPT = 2
SPILT = NT - KEPT
EPS = 1e-5
QMIN = 1e-8
MAGIC = 1.5 * 2.0 ** 23
NEG = float(np.finfo(np.float32).min)
RSQRT_SEED = float(0x5F3759DF)
LN_OPS = 20


def constants():
    half = D // 2
    inv = (1.0 / np.float32(10000.0) ** (np.arange(half, dtype=np.float32) / np.float32(half))).astype(np.float32)
    ang = np.arange(S, dtype=np.float32)[None, :] * inv[:, None]
    cos, sin = np.cos(ang).astype(np.float32), np.sin(ang).astype(np.float32)
    lay = lambda a: np.ascontiguousarray(a.reshape(2, P, S).transpose(1, 0, 2).reshape(P, 2 * S).astype(np.float32))
    root = np.float32(np.sqrt(DK))
    rope = np.stack([lay(cos * root), lay(sin * root), lay(cos), lay(sin)], 1)
    q, k = np.arange(S)[:, None], np.arange(S)[None, :]
    mask = np.where(np.abs(q - k) <= WINDOW, 0.0, NEG).astype(np.float32)
    mask = np.ascontiguousarray(mask.reshape(2, P, S).transpose(1, 0, 2))
    sel = np.zeros((P // DK, 2 * H, H, P), np.float32)
    for h in range(H):
        sel[:, h, h] = sel[:, H + h, h] = 1.0
    sel = sel.reshape(P, H, P)
    return {"c_rope": rope, "c_mask": mask, "c_sel": sel, "c_ident": np.eye(P, dtype=np.float32)}


def build(nc, t):
    x_d, ctx_d, out_d = t["x"], t["ctxT"], t["out"]
    x_rows = x_d.rearrange("(n s p) d -> n p s d", p=P, s=2)
    ctx_cols = ctx_d.rearrange("(c p) t -> p c t", p=P)
    x1_d = nc.dram_tensor("x1_scratch", [TOK, D], F32, kind="Internal").ap()
    x1_rows = x1_d.rearrange("(n s p) d -> n p s d", p=P, s=2)
    x1_tiles = x1_d.rearrange("(n u p) d -> n p u d", p=P, u=SUB)
    out_tiles = out_d.rearrange("(n u p) d -> n p u d", p=P, u=SUB)
    hid_d = nc.dram_tensor("hidden_scratch", [SPILT * FC, P, TT], F32, kind="Internal").ap()
    win_rows = t["winT"].rearrange("(j p) d -> j p d", p=P)
    wout_rows = t["wout"].rearrange("(j p) d -> j p d", p=P)

    with ExitStack() as ctx:
        def sem(name):
            return ctx.enter_context(nc.semaphore(name))

        def sb(name, shape, dt=F32, where=ctx):
            return where.enter_context(nc.sbuf_tensor(name, shape, dt))

        win_int = sb("win_int", [P, KC, FF], BF16)
        ident = sb("ident", [P, P])
        ident_b = sb("ident_b", [P, P], BF16)
        ln2_r = sb("ln2_r", [P, 2 * NB])
        ln2_b = sb("ln2_b", [P, 2 * NB])
        ymax = sb("ymax", [P, 2 * NB])
        win_amax = sb("win_amax", [P, FC])
        b_in = sb("b_in", [P, FC])
        tiny = sb("tiny", [P, 8])
        magic_c = sb("magic_c", [P, 1])
        ones = sb("ones", [P, DK])

        pa = ExitStack()
        w_hi, w_lo = {}, {}
        for n in ("wv", "wq", "wk", "wo"):
            w_hi[n] = sb(n + "_hi", [P, KC, D], F32R, pa)
            w_lo[n] = sb(n + "_lo", [P, KC, D], F32R, pa)
        rope = sb("rope", [P, 4, 2, S], F32, pa)
        mask = sb("mask", [P, 2, S], F32, pa)
        sel = sb("sel", [P, H, P], F32R, pa)
        wo_b = sb("wo_b", [P, D], F32, pa)
        q_hi = sb("q_hi", [P, 2, KC, S], F32R, pa)
        q_lo = sb("q_lo", [P, 2, KC, S], F32R, pa)
        k_hi = sb("k_hi", [P, 2, KC, S], F32R, pa)
        k_lo = sb("k_lo", [P, 2, KC, S], F32R, pa)
        v_sb = sb("v_sb", [P, 2, 2, D], F32, pa)
        probs = sb("probs", [P, 4, 2, S], F32, pa)
        xT_hi = sb("xT_hi", [P, KC, S], F32R, pa)
        xT_lo = sb("xT_lo", [P, KC, S], F32R, pa)
        ctx_raw = sb("ctx_raw", [P, KC, S], F32, pa)
        cT_hi = sb("cT_hi", [P, KC, S], F32R, pa)
        cT_lo = sb("cT_lo", [P, KC, S], F32R, pa)
        o_f = sb("o_f", [P, S], F32, pa)
        o_rec = sb("o_rec", [P, S], F32, pa)
        o_hi = sb("o_hi", [P, KC, S], F32R, pa)
        o_lo = sb("o_lo", [P, KC, S], F32R, pa)
        x_ln = sb("x_ln", [P, 2, D], F32, pa)
        x_res = sb("x_res", [P, 2, D], F32, pa)
        rt = sb("rt", [P, 2, 2, S], F32, pa)
        roped = sb("roped", [P, 2, KC, S], F32, pa)
        w_raw = sb("w_raw", [P, D], F32, pa)
        w_q = sb("w_q", [P, D], BF16, pa)
        y2 = sb("y2", [P, D], F32, pa)
        row_max = sb("row_max", [P, 2, H], F32, pa)
        neg_max = sb("neg_max", [P, 2, ROWT, 2 * H], F32, pa)
        mT = sb("mT", [P, S], F32R, pa)
        bn = sb("bn", [P, 2, 2, 6], F32, pa)
        mv = sb("mv", [P, 2, 2, 2], F32, pa)
        veps = sb("veps", [P, 2, 2], F32, pa)
        rstd = sb("rstd", [P, 2, 2], F32, pa)
        nt_t = sb("nt_t", [P, 2, 2], F32, pa)
        nmr = sb("nmr", [P, 2, 2], F32, pa)
        w_s = sb("w_s", [P, 4], F32, pa)
        pa.close()

        pb = ExitStack()
        wout_int = sb("wout_int", [P, FC, D], BF16, pb)
        h_kept = sb("h_kept", [P, KEPT * FC, TT], F32, pb)
        xq = sb("xq", [P, 2, SUB, D], F32, pb)
        qT_hi = sb("qT_hi", [P, 2, KC, TT], BF16, pb)
        qT_lo = sb("qT_lo", [P, 2, KC, TT], BF16, pb)
        h_ring = sb("h_ring", [P, 4, TT], F32, pb)
        wo_raw = sb("wo_raw", [P, 2, D], F32, pb)
        b_out = sb("b_out", [P, D], F32, pb)
        hmax = sb("hmax", [P, NT * FC], F32, pb)
        x_a = sb("x_a", [P, 2 * NB], F32, pb)
        x_b = sb("x_b", [P, 2 * NB], F32, pb)
        g_scale = sb("g_scale", [P, FC], F32, pb)
        wout_amax = sb("wout_amax", [P, FC], F32, pb)
        wout_pow = sb("wout_pow", [P, FC], F32, pb)
        wout_man = sb("wout_man", [P, FC], F32, pb)
        wp_s = sb("wp_s", [P, 2, 4], F32, pb)
        h_int = sb("h_int", [P, 4, TT], F32, pb)
        g_hi = sb("g_hi", [P, 4, TT], F16, pb)
        g_lo = sb("g_lo", [P, 4, TT], F16, pb)
        o_out = sb("o_out", [P, 2, D], F32, pb)
        pb.close()

        bank = [ctx.enter_context(nc.psum_tensor(f"bank{i}", [P, 512], F32)) for i in range(8)]
        ring = bank[0:3]
        p3, p4, p5 = bank[3:6]
        pv_bank = bank[6:8]

        c_in, sel_in, b_out_in = sem("c_in"), sem("sel_in"), sem("b_out_in")
        w_in = {n: sem("in_" + n) for n in ("wv", "wq", "wk", "wo")}
        w_hi_done, w_lo_done, ones_done = sem("w_hi_done"), sem("w_lo_done"), sem("ones_done")
        ctx_in, xln_in, xres_in, win_in, x1_out = (sem(n) for n in ("ctx_in", "xln_in", "xres_in", "win_in", "x1_out"))
        ln1_chain, ln1_norm = sem("ln1_chain"), sem("ln1_norm")
        ln2_chain, ln2_stats, y2_done, ymax_done = sem("ln2_chain"), sem("ln2_stats"), sem("y2_done"), sem("ymax_done")
        xt_mm, xt_hi, xt_lo = sem("xt_mm"), sem("xt_hi"), sem("xt_lo")
        c_hi, c_lo = sem("c_hi"), sem("c_lo")
        v_mm, q_mm, k_mm, o_mm = sem("v_mm"), sem("q_mm"), sem("k_mm"), sem("o_mm")
        v_done = sem("v_done")
        rope_step = {"q": sem("rope_q_step"), "k": sem("rope_k_step")}
        hi_done = {"q": sem("q_hi_done"), "k": sem("k_hi_done")}
        lo_done = {"q": sem("q_lo_done"), "k": sem("k_lo_done")}
        s_mm, max_done, msplit, mT_mm, mT_done = (sem(n) for n in ("s_mm", "max_done", "msplit", "mT_mm", "mT_done"))
        st_mm, exp_done, p_ready, pv_mm = sem("st_mm"), sem("exp_done"), sem("p_ready"), sem("pv_mm")
        rec_done, onorm, ohi_done, olo_done = sem("rec_done"), sem("onorm"), sem("ohi_done"), sem("olo_done")
        xres_b, res_done = sem("xres_b"), sem("res_done")
        wq_chain, wt_mm, wt_done = sem("wq_chain"), sem("wt_mm"), sem("wt_done")
        a_done = sem("a_done")
        passed = sem("passed")

        b_in_sem = [sem(f"xq_in{i}") for i in range(2)]
        wo_raw_in = [sem(f"wo_raw_in{i}") for i in range(2)]
        bset, bset_pool = sem("bset"), sem("bset_pool")
        z_done, z_round, qt_mm, qt_hi, qt_lo = (sem(n) for n in ("z_done", "z_round", "qt_mm", "qt_hi", "qt_lo"))
        h_mm, gelu_done, hmax_done = sem("h_mm"), sem("gelu_done"), sem("hmax_done")
        h_out = [sem(f"h_out{i}") for i in range(4)]
        wo_chain = sem("wo_chain")
        cset, cset_pool = sem("cset"), sem("cset_pool")
        h_in = [sem(f"h_in{i}") for i in range(4)]
        xc_in = [sem(f"xc_in{i}") for i in range(2)]
        xc_b = sem("xc_b")
        hint_done, g_done, ghi_done, glo_done, y_mm, y_done = (
            sem(n) for n in ("hint_done", "g_done", "ghi_done", "glo_done", "y_mm", "y_done"))
        y_out = [sem(f"y_out{i}") for i in range(2)]

        ROPE_OPS = 6
        WQ_OPS = 7
        WO_OPS = 8
        NCONST = 6

        def steps(e, step):
            step(0, 0, False, True, True)
            step(1, 1, True, True, True)
            with e.Fori(1, NB // 2 - 1) as i:
                step(2 * i, 0, True, True, True)
                step(2 * i + 1, 1, True, True, True)
            step(NB - 2, 0, True, True, False)
            step(NB - 1, 1, True, False, False)

        def wait(e, s, value):
            if isinstance(value, int) and value <= 0:
                return
            e.wait_ge(s, value)

        def chain(e, s, base):
            n = [0]

            def link(ins):
                n[0] += 1
                ins.then_inc(s, 1)
                e.wait_ge(s, base + n[0])
            link.count = n
            return link

        def apart(e):
            e.sem_inc(passed, 1)

        block = ctx.enter_context(nc.Block())

        @block.sync
        def _(sp):
            def load_ctx(j):
                if not (isinstance(j, int) and j == 0):
                    sp.wait_ge(c_hi, j)
                    sp.wait_ge(c_lo, j)
                sp.dma_start(ctx_raw[:], ctx_cols[:, :, bass.ds(j * S, S)]).then_inc(ctx_in, 16)

            def load_xln(j):
                wait(sp, xt_mm, 2 * j)
                sp.dma_start(x_ln[:], x_rows[bass.ds(j, 1)].rearrange("o p s d -> p (o s) d")).then_inc(xln_in, 16)

            def load_xres(j):
                wait(sp, x1_out, 16 * j)
                apart(sp)
                wait(sp, y2_done, 2 * j)
                sp.dma_start(x_res[:], x_rows[bass.ds(j, 1)].rearrange("o p s d -> p (o s) d")).then_inc(xres_in, 16)

            def store_x1(j):
                sp.wait_ge(res_done, 2 * j + 2)
                sp.dma_start(x1_rows[bass.ds(j, 1)].rearrange("o p s d -> p (o s) d"), x_res[:]).then_inc(x1_out, 16)

            def load_win(j):
                wait(sp, wq_chain, WQ_OPS * j)
                sp.dma_start(w_raw[:], win_rows[bass.ds(j, 1)].rearrange("o p d -> p (o d)")).then_inc(win_in, 16)

            wsrc = {n: t[n].rearrange("(c p) e -> p c e", p=P) for n in ("wv", "wq", "wk", "wo")}
            load_xln(0)
            sp.dma_start(ident[:], t["c_ident"]).then_inc(c_in, 16)
            load_ctx(0)
            sp.dma_start(v_sb[:].rearrange("p a b d -> p (a b) d"), wsrc["wv"]).then_inc(w_in["wv"], 16)
            sp.dma_start(roped[:].rearrange("p a c s -> p (a c s)"), wsrc["wq"]).then_inc(w_in["wq"], 16)
            sp.dma_start(rope[:].rearrange("p a b s -> p a (b s)"), t["c_rope"]).then_inc(c_in, 16)
            sp.dma_start(mask[:], t["c_mask"]).then_inc(c_in, 16)
            sp.dma_start(wo_b[:], t["wo_b"]).then_inc(c_in, 16)
            sp.dma_start(b_in[:], t["b_in"]).then_inc(c_in, 16)
            sp.wait_ge(w_hi_done, 1)
            sp.wait_ge(w_lo_done, 1)
            sp.dma_start(v_sb[:].rearrange("p a b d -> p (a b) d"), wsrc["wk"]).then_inc(w_in["wk"], 16)
            sp.wait_ge(w_hi_done, 2)
            sp.wait_ge(w_lo_done, 2)
            sp.dma_start(roped[:].rearrange("p a c s -> p (a c s)"), wsrc["wo"]).then_inc(w_in["wo"], 16)
            load_ctx(1)
            load_xln(1)
            load_xres(0)
            load_win(0)
            load_xln(2)

            def step(b, par, has_o, has_proj, has_xt):
                if has_xt:
                    load_ctx(b + 2)
                if has_proj:
                    load_win(b + 1)
                if has_o:
                    store_x1(b - 1)
                    load_xres(b)
                if not (isinstance(b, int) and b + 3 >= NB) and has_xt:
                    load_xln(b + 3)

            step(0, 0, False, True, True)
            step(1, 1, True, True, True)
            with sp.Fori(1, NB // 2 - 2) as i:
                step(2 * i, 0, True, True, True)
                step(2 * i + 1, 1, True, True, True)
            step(NB - 4, 0, True, True, True)
            step(NB - 3, 1, True, True, True)
            step(NB - 2, 0, True, True, False)
            step(NB - 1, 1, True, False, False)
            store_x1(NB - 1)
            sp.wait_ge(x1_out, 16 * NB)
            sp.wait_ge(a_done, 4)
            sp.dma_start(b_out[:], t["b_out"]).then_inc(b_out_in, 16)

            def load_xq(n, par):
                wait(sp, qt_mm, n - 1)
                sp.dma_start(xq[:, par], x1_tiles[bass.ds(n, 1)].rearrange("o p u d -> p (o u) d")).then_inc(b_in_sem[par], 16)

            def load_wout(j, par):
                wait(sp, wo_chain, WO_OPS * (j - 1))
                sp.dma_start(wo_raw[:, par], wout_rows[bass.ds(j, 1)].rearrange("o p d -> p (o d)")).then_inc(wo_raw_in[par], 16)

            def store_hidden(n):
                for f in range(FC):
                    sp.wait_ge(gelu_done, FC * n + f + 1)
                    sp.dma_start(hid_d[bass.ds(FC * n + f, 1)].rearrange("o p t -> p (o t)"), h_ring[:, f % 4]).then_inc(h_out[f % 4], 16)

            def tile_b(n, par, spilt, more):
                load_wout(2 * n, 0)
                load_wout(2 * n + 1, 1)
                if spilt:
                    store_hidden(n)
                if more:
                    load_xq(n + 2, par)

            load_xq(0, 0)
            load_xq(1, 1)
            tile_b(0, 0, True, True)
            tile_b(1, 1, True, True)
            with sp.Fori(1, SPILT // 2) as i:
                tile_b(2 * i, 0, True, True)
                tile_b(2 * i + 1, 1, True, True)
            for n in range(SPILT, NT):
                tile_b(n, n % 2, False, n + 2 < NT)

            def load_xc(i, par, tile):
                wait(sp, qt_mm, NT)
                wait(sp, y_done, SUB * (i - 1))
                sp.dma_start(xq[:, par], x1_tiles[bass.ds(tile, 1)].rearrange("o p u d -> p (o u) d")).then_inc(xc_in[par], 16)

            def store_y(i, tile):
                for u in range(SUB):
                    sp.wait_ge(y_done, SUB * i + u + 1)
                    sp.dma_start(out_tiles[bass.ds(tile, 1), :, u].rearrange("o p d -> p (o d)"), o_out[:, u % 2]).then_inc(y_out[u % 2], 16)

            load_xc(0, 0, SPILT)
            load_xc(1, 1, SPILT + 1)
            for i in range(KEPT):
                store_y(i, SPILT + i)
                load_xc(i + 2, i % 2, SPILT + i + 2 if i + 2 < KEPT else i + 2 - KEPT)
            for i in range(SPILT):
                store_y(KEPT + i, i)
                if i + 2 < SPILT:
                    load_xc(KEPT + i + 2, i % 2, i + 2)
            for q in y_out:
                sp.wait_ge(q, 16 * NT * SUB // 2)

        @block.tensor
        def _(pe):
            def split3(out, lhs, rhs, first, last):
                (l_hi, l_lo), (r_hi, r_lo) = lhs, rhs
                pe.matmul(out, l_hi, r_hi, start=first, stop=False)
                pe.matmul(out, l_hi, r_lo, start=False, stop=False)
                return pe.matmul(out, l_lo, r_hi, start=False, stop=last)

            def x_transposes(j, s):
                dst = (p3, p4)[s]
                if s == 0:
                    pe.wait_ge(ln1_norm, 2 * j + 2)
                wait(pe, rope_step["k"], ROPE_OPS * (j - 1))
                for c in range(KC):
                    mm = pe.transpose(dst[:, c * P:(c + 1) * P], x_ln[:, s, c * P:(c + 1) * P], ident[:])
                mm.then_inc(xt_mm, 1)

            def v_tile(j, s, has_o, has_wt):
                if s == 0:
                    pe.wait_ge(c_hi, j + 1)
                    pe.wait_ge(c_lo, j + 1)
                    if has_wt:
                        wait(pe, wt_done, j - 1)
                    wait(pe, rope_step["q"], ROPE_OPS * j)
                elif has_o:
                    pe.wait_ge(res_done, 2 * (j - 2) + 1)
                else:
                    pe.wait_ge(xt_hi, 2 * j + 1)
                    pe.wait_ge(xt_lo, 2 * j + 1)
                dst = (p5, p3)[s]
                for c in range(KC):
                    tok = slice(s * P, (s + 1) * P)
                    mm = split3(dst[:], (cT_hi[:, c, tok], cT_lo[:, c, tok]),
                                (w_hi["wv"][:, c], w_lo["wv"][:, c]), c == 0, c == KC - 1)
                mm.then_inc(v_mm, 1)

            def qk_tile(j, which, half, has_o):
                src = (xT_hi, xT_lo) if which == "q" else (cT_hi, cT_lo)
                if which == "q" and half == 0:
                    pe.wait_ge(xt_hi, 2 * j + 2)
                    pe.wait_ge(xt_lo, 2 * j + 2)
                    if has_o:
                        pe.wait_ge(res_done, 2 * (j - 2) + 2)
                elif which == "q":
                    pe.wait_ge(v_done, 2 * j + 1)
                elif half == 0:
                    pe.wait_ge(v_done, 2 * j + 2)
                else:
                    pe.wait_ge(rope_step["q"], ROPE_OPS * (j + 1))
                dst = {"q": (p4, p5), "k": (p3, p4)}[which][half]
                w = "w" + which
                for a in range(2):
                    e = slice((2 * half + a) * P, (2 * half + a + 1) * P)
                    for c in range(KC):
                        mm = split3(dst[:, a * S:(a + 1) * S], (w_hi[w][:, c, e], w_lo[w][:, c, e]),
                                    (src[0][:, c], src[1][:, c]), c == 0, c == KC - 1)
                mm.then_inc(q_mm if which == "q" else k_mm, 1)

            def o_tile(j, s, has_xt):
                if s == 0:
                    pe.wait_ge(ohi_done, KC * (j + 1))
                    pe.wait_ge(olo_done, KC * (j + 1))
                    pe.wait_ge(w_hi_done, 4)
                    pe.wait_ge(w_lo_done, 4)
                if has_xt:
                    pe.wait_ge(xt_hi, 2 * (j + 2) + s + 1)
                    pe.wait_ge(xt_lo, 2 * (j + 2) + s + 1)
                elif s == 0:
                    pe.wait_ge(rope_step["k"], ROPE_OPS * NB)
                dst = (p3, p4)[s]
                for c in range(KC):
                    tok = slice(s * P, (s + 1) * P)
                    mm = split3(dst[:], (o_hi[:, c, tok], o_lo[:, c, tok]),
                                (w_hi["wo"][:, c], w_lo["wo"][:, c]), c == 0, c == KC - 1)
                mm.then_inc(o_mm, 1)

            def scores(b, par, h):
                c, r = h // NC4, slice(DK * (h % NC4), DK * (h % NC4) + DK)
                if h == 0:
                    for n in ("q", "k"):
                        pe.wait_ge(hi_done[n], b + 1)
                if h < 3:
                    wait(pe, exp_done, H * b)
                else:
                    pe.wait_ge(max_done, 2 * H * b + 2 * (h - 2))
                for qb in range(2):
                    mm = pe.matmul(ring[h % 3][:, qb * S:(qb + 1) * S], q_hi[r, par, c, qb * P:(qb + 1) * P],
                                   k_hi[r, par, c], start=True, stop=True)
                mm.then_inc(s_mm, 1)

            def max_transposes(b):
                pe.wait_ge(msplit, 4 * (b + 1))
                wait(pe, onorm, KC * b)
                for qb in range(2):
                    mm = pe.transpose(pv_bank[0][:, qb * P:(qb + 1) * P], neg_max[:, qb].rearrange("p r h -> p (r h)"), ident[:])
                mm.then_inc(mT_mm, 1)

            def scores_t(b, par, h):
                c, r = h // NC4, slice(DK * (h % NC4), DK * (h % NC4) + DK)
                if h == 0:
                    pe.wait_ge(mT_done, b + 1)
                    for n in ("q", "k"):
                        pe.wait_ge(lo_done[n], 2 * (b + 1))
                if h < 3:
                    pe.wait_ge(max_done, 2 * H * (b + 1))
                else:
                    pe.wait_ge(exp_done, H * b + h - 2)
                for kb in range(2):
                    out, keys = ring[h % 3][:, kb * S:(kb + 1) * S], slice(kb * P, (kb + 1) * P)
                    split3(out, (k_hi[r, par, c, keys], k_lo[r, par, c, keys]), (q_hi[r, par, c], q_lo[r, par, c]), True, False)
                    mm = pe.matmul(out, sel[r, h], mT[r], start=False, stop=True)
                mm.then_inc(st_mm, 1)

            def weighted(b, par, h):
                c, r = h // NC4, slice(DK * (h % NC4), DK * (h % NC4) + DK)
                pe.wait_ge(p_ready, 2 * (H * b + h + 1))
                if h % NC4 == 0:
                    wait(pe, onorm, KC * b + c - 1)
                    if h == 0:
                        pe.wait_ge(v_done, 2 * (b + 1))
                out = pv_bank[c % 2]
                for kb in range(2):
                    pe.matmul(out[r, 0:S], v_sb[:, par, kb, h * DK:(h + 1) * DK], probs[:, h % 4, kb],
                              start=kb == 0, stop=kb == 1)
                for kb in range(2):
                    mm = pe.matmul(out[r, S:2 * S], ones[:], probs[:, h % 4, kb], start=kb == 0, stop=kb == 1)
                mm.then_inc(pv_mm, 1)

            def w_transposes(b):
                pe.wait_ge(wq_chain, WQ_OPS * (b + 1))
                dst = p5[:].bitcast(BF16)
                for c in range(KC):
                    mm = pe.transpose(dst[:, c * P:(c + 1) * P], w_q[:, c * P:(c + 1) * P], ident_b[:])
                mm.then_inc(wt_mm, 1)

            pe.wait_ge(sel_in, 16)
            pe.wait_ge(ones_done, 3)
            pe.wait_ge(w_hi_done, 3)
            pe.wait_ge(w_lo_done, 3)
            x_transposes(0, 0)
            x_transposes(0, 1)
            v_tile(0, 0, False, False)
            v_tile(0, 1, False, False)
            for which in ("q", "k"):
                for half in range(2):
                    qk_tile(0, which, half, False)
            x_transposes(1, 0)
            x_transposes(1, 1)

            LAG = 3

            def step(b, par, has_o, has_proj, has_xt):
                tiles = []
                if has_o:
                    tiles += [lambda: o_tile(b - 1, 0, has_proj), lambda: o_tile(b - 1, 1, has_proj)]
                if has_proj:
                    tiles += [lambda: v_tile(b + 1, 0, has_o, True), lambda: v_tile(b + 1, 1, has_o, True),
                              lambda: qk_tile(b + 1, "q", 0, has_o), lambda: qk_tile(b + 1, "q", 1, has_o)]
                h = 0
                for n, tile in enumerate(tiles):
                    for _ in range(3 if n < 2 else 2):
                        scores(b, par, h)
                        h += 1
                    tile()
                while h < H:
                    scores(b, par, h)
                    h += 1
                if has_proj:
                    qk_tile(b + 1, "k", 0, has_o)
                max_transposes(b)
                if has_proj:
                    qk_tile(b + 1, "k", 1, has_o)
                for h in range(H + LAG):
                    if h < H:
                        scores_t(b, par, h)
                    if h >= LAG:
                        weighted(b, par, h - LAG)
                    if h == 10:
                        w_transposes(b)
                        if has_xt:
                            x_transposes(b + 2, 0)
                            x_transposes(b + 2, 1)

            steps(pe, step)
            o_tile(NB - 1, 0, False)
            o_tile(NB - 1, 1, False)
            pe.wait_ge(res_done, 2 * NB)
            pe.wait_ge(wt_done, NB)
            pe.wait_ge(onorm, KC * NB)
            pe.drain().then_inc(a_done, 1)
            pe.wait_ge(a_done, 4)

            def q_transposes(n, par):
                for u in range(SUB):
                    pe.wait_ge(z_round, SUB * n + u + 1)
                    if u == 0:
                        wait(pe, qt_lo, KC * n)
                        wait(pe, qt_hi, KC * n)
                    for c in range(KC):
                        mm = pe.transpose(bank[4 + c][:, u * P:(u + 1) * P], xq[:, par, u, c * P:(c + 1) * P], ident[:])
                mm.then_inc(qt_mm, 1)

            def hidden_chunk(n, par, f):
                if f == 0:
                    pe.wait_ge(qt_hi, KC * (n + 1))
                    pe.wait_ge(qt_lo, KC * (n + 1))
                wait(pe, gelu_done, FC * n + f - 3)
                for c in range(KC):
                    for part in (qT_hi, qT_lo):
                        mm = pe.matmul(bank[f % 4][:], win_int[:, c, f * P:(f + 1) * P], part[:, par, c],
                                       start=c == 0 and part is qT_hi, stop=c == KC - 1 and part is qT_lo)
                mm.then_inc(h_mm, 1)

            def tile_b(n, par, more):
                for f in range(FC):
                    hidden_chunk(n, par, f)
                    if f == 9 and more:
                        q_transposes(n + 1, 1 - par)

            q_transposes(0, 0)
            tile_b(0, 0, True)
            tile_b(1, 1, True)
            with pe.Fori(1, SPILT // 2) as i:
                tile_b(2 * i, 0, True)
                tile_b(2 * i + 1, 1, True)
            for n in range(SPILT, NT):
                tile_b(n, n % 2, n + 1 < NT)

            pe.wait_ge(wo_chain, WO_OPS * FC)
            pe.wait_ge(gelu_done, FC * NT)

            def tile_c(i, par):
                wait(pe, y_done, SUB * (i - 1))
                for f in range(FC):
                    pe.wait_ge(ghi_done, FC * i + f + 1)
                    pe.wait_ge(glo_done, FC * i + f + 1)
                    for u in range(SUB):
                        for part in (g_hi, g_lo):
                            mm = pe.matmul(bank[4 * par + u][:], part[:, f % 4, u * P:(u + 1) * P], wout_int[:, f],
                                           start=f == 0 and part is g_hi, stop=f == FC - 1 and part is g_lo)
                    mm.then_inc(y_mm, 1)

            tile_c(0, 0)
            tile_c(1, 1)
            with pe.Fori(1, NT // 2) as i:
                tile_c(2 * i, 0)
                tile_c(2 * i + 1, 1)

        @block.scalar
        def _(act):
            def split_hi(which, j):
                par = j_par[0]
                src, dst = (0, q_hi) if which == "q" else (1, k_hi)
                act.wait_ge(rope_step[which], ROPE_OPS * (j + 1))
                act.copy(dst[:, par], roped[:, src]).then_inc(hi_done[which], 1)

            j_par = [0]

            def ctx_hi(j):
                act.wait_ge(ctx_in, 16 * (j + 1))
                wait(act, k_mm, 2 * j)
                act.copy(cT_hi[:], ctx_raw[:]).then_inc(c_hi, 1)

            def norm1(j):
                act.wait_ge(ln1_chain, LN_OPS * (j + 1))
                for s in range(2):
                    act.activation(x_ln[:, s], x_ln[:, s], ACT.Identity, bias=nmr[:, 0, s:s + 1],
                                   scale=rstd[:, 0, s:s + 1]).then_inc(ln1_norm, 1)

            def xt_lead(j, s):
                act.wait_ge(xt_mm, 2 * j + s + 1)
                act.copy(xT_hi[:, :, s * P:(s + 1) * P], (p3, p4)[s][:].rearrange("p (c t) -> p c t", c=KC)).then_inc(xt_hi, 1)

            def v_copy(j, par, s):
                act.wait_ge(v_mm, 2 * j + s + 1)
                act.copy(v_sb[:, par, s], (p5, p3)[s][:]).then_inc(v_done, 1)

            def norm2(j, s):
                if s == 0:
                    act.wait_ge(ln2_stats, j + 1)
                wait(act, ymax_done, 2 * j + s)
                act.activation(y2[:], x_res[:, s], ACT.Identity, bias=nmr[:, 1, s:s + 1],
                               scale=rstd[:, 1, s:s + 1]).then_inc(y2_done, 1)

            def softmax_exp(b, h):
                act.wait_ge(st_mm, H * b + h + 1)
                wait(act, pv_mm, H * b + h - 3)
                act.activation(probs[:, h % 4].rearrange("p k q -> p (k q)"), ring[h % 3][:], ACT.Exp).then_inc(exp_done, 1)

            def out_hi(b, c):
                act.wait_ge(onorm, KC * b + c + 1)
                act.copy(o_hi[:, c], o_f[:]).then_inc(ohi_done, 1)

            act.wait_ge(xln_in, 16)
            norm1(0)
            stage = {"wv": v_sb[:].rearrange("p a b d -> p (a b) d"), "wk": v_sb[:].rearrange("p a b d -> p (a b) d"),
                     "wq": roped[:].rearrange("p a c s -> p (a c s)").rearrange("p (c e) -> p c e", c=KC),
                     "wo": roped[:].rearrange("p a c s -> p (a c s)").rearrange("p (c e) -> p c e", c=KC)}
            ctx_hi(0)
            for n in ("wv", "wq", "wk", "wo"):
                act.wait_ge(w_in[n], 16)
                act.copy(w_hi[n][:], stage[n]).then_inc(w_hi_done, 1)
            xt_lead(0, 0)
            xt_lead(0, 1)
            v_copy(0, 0, 0)
            act.wait_ge(w_lo_done, 3)
            v_copy(0, 0, 1)
            norm1(1)
            j_par[0] = 0
            split_hi("q", 0)
            split_hi("k", 0)
            ctx_hi(1)
            xt_lead(1, 0)
            xt_lead(1, 1)

            def step(b, par, has_o, has_proj, has_xt):
                j_par[0] = 1 - par
                if has_o:
                    norm2(b - 1, 0)
                if has_proj:
                    v_copy(b + 1, 1 - par, 0)
                if has_o:
                    norm2(b - 1, 1)
                if has_proj:
                    v_copy(b + 1, 1 - par, 1)
                act.wait_ge(mT_mm, b + 1)
                act.copy(mT[:], pv_bank[0][:, 0:S]).then_inc(mT_done, 1)
                for h in range(H):
                    softmax_exp(b, h)
                    if h == 1 and has_proj:
                        split_hi("q", b + 1)
                    if h == 4 and has_proj:
                        split_hi("k", b + 1)
                    if h == 5 and has_xt:
                        ctx_hi(b + 2)
                    if h == 7 and has_xt:
                        norm1(b + 2)
                    if h in (9, 13):
                        out_hi(b, (h - 9) // 4)
                    if h == 11:
                        act.wait_ge(wt_mm, b + 1)
                        act.copy(win_int[:, :, bass.ds(b * P, P)],
                                 p5[:].bitcast(BF16)[:, 0:D].rearrange("p (c f) -> p c f", c=KC)).then_inc(wt_done, 1)
                        if has_xt:
                            xt_lead(b + 2, 0)
                            xt_lead(b + 2, 1)
                out_hi(b, 2)
                out_hi(b, 3)

            steps(act, step)
            norm2(NB - 1, 0)
            norm2(NB - 1, 1)
            act.wait_ge(y2_done, 2 * NB)
            act.drain().then_inc(a_done, 1)
            act.wait_ge(a_done, 4)

            act.wait_ge(bset, 7)

            def scale_tile(n, par):
                act.wait_ge(b_in_sem[par], 8 * n + (16 if par == 0 else 8))
                for u in range(SUB):
                    col = bass.ds(SUB * n + u, 1)
                    act.activation(xq[:, par, u], xq[:, par, u], ACT.Identity, bias=x_b[:, col],
                                   scale=x_a[:, col]).then_inc(z_done, 1)

            def lead(n, par):
                act.wait_ge(qt_mm, n + 1)
                for c in range(KC):
                    act.copy(qT_hi[:, par, c], bank[4 + c][:]).then_inc(qt_hi, 1)

            def tile_b(n, par, spilt, more):
                for f in range(FC):
                    act.wait_ge(h_mm, FC * n + f + 1)
                    if spilt:
                        if f < 4:
                            wait(act, h_out[f], 64 * n)
                            wait(act, hmax_done, FC * n + f - 3)
                        else:
                            act.wait_ge(h_out[f % 4], 64 * n + 16 * (f // 4))
                            act.wait_ge(hmax_done, FC * n + f - 3)
                        dst = h_ring[:, f % 4]
                    else:
                        dst = h_kept[:, (n - SPILT) * FC + f]
                    act.activation(dst, bank[f % 4][:], ACT.Gelu, bias=b_in[:, f:f + 1],
                                   scale=g_scale[:, f:f + 1]).then_inc(gelu_done, 1)
                    if f == 4 and more:
                        scale_tile(n + 1, 1 - par)
                    if f == 11 and more:
                        lead(n + 1, 1 - par)

            scale_tile(0, 0)
            lead(0, 0)
            tile_b(0, 0, True, True)
            tile_b(1, 1, True, True)
            with act.Fori(1, SPILT // 2) as i:
                tile_b(2 * i, 0, True, True)
                tile_b(2 * i + 1, 1, True, True)
            for n in range(SPILT, NT):
                tile_b(n, n % 2, False, n + 1 < NT)

            act.wait_ge(cset, 4)

            def load_hidden(n, f):
                act.dma_start(h_ring[:, f % 4], hid_d[bass.ds(FC * n + f, 1)].rearrange("o p t -> p (o t)")).then_inc(h_in[f % 4], 16)

            for q in h_out:
                act.wait_ge(q, 16 * SPILT * FC // 4)
            for f in range(4):
                load_hidden(0, f)

            def lead_c(i, f):
                act.wait_ge(g_done, FC * i + f + 1)
                if f >= 4:
                    act.wait_ge(y_mm, FC * i + f - 3)
                else:
                    wait(act, y_mm, FC * i + f - 3)
                act.copy(g_hi[:, f % 4], h_int[:, f % 4]).then_inc(ghi_done, 1)

            def tile_c(i, src, spilt, more):
                for f in range(FC + 1):
                    if f < FC:
                        if spilt:
                            act.wait_ge(h_in[f % 4], 64 * src + 16 * (f // 4) + 16)
                        wait(act, glo_done, FC * i + f - 3)
                        wait(act, ghi_done, FC * i + f - 3)
                        chunk = h_ring[:, f % 4] if spilt else h_kept[:, FC * src + f]
                        act.activation(h_int[:, f % 4], chunk, ACT.Identity, bias=magic_c[:], scale=tiny[:, 5:6]).then_inc(hint_done, 1)
                    if f >= 1:
                        lead_c(i, f - 1)
                        if spilt and (more or f - 1 + 4 < FC):
                            act.wait_ge(hint_done, FC * i + f)
                            n, g = (src, f + 3) if f + 3 < FC else (src + 1, f + 3 - FC)
                            load_hidden(n, g)

            for i in range(KEPT):
                tile_c(i, i, False, True)
            with act.Fori(0, SPILT - 1) as i:
                tile_c(KEPT + i, i, True, True)
            tile_c(NT - 1, SPILT - 1, True, False)

        @block.vector
        def _(dve):
            def rsqrt(link, v, r, tmp):
                link(dve.tensor_scalar(r.bitcast(I32), v.bitcast(I32), 1, None, ALU.logical_shift_right))
                link(dve.tensor_scalar(r.bitcast(I32), r.bitcast(I32), -1.0, RSQRT_SEED, ALU.mult, ALU.add))
                for _ in range(3):
                    link(dve.tensor_tensor(tmp, r, r, ALU.mult))
                    link(dve.tensor_tensor(tmp, tmp, v, ALU.mult))
                    link(dve.tensor_scalar(tmp, tmp, -0.5, 1.5, ALU.mult, ALU.add))
                    link(dve.tensor_tensor(r, r, tmp, ALU.mult))

            def ln_stats(link, src, which):
                for s in range(2):
                    link(dve.bn_stats(bn[:, which, s], src[:, s]))
                for s in range(2):
                    apart(dve)
                    link(dve.bn_aggr(mv[:, which, s], bn[:, which, s]))
                link(dve.tensor_scalar(veps[:, which], mv[:, which, :, 1], EPS, None, ALU.add))
                rsqrt(link, veps[:, which], rstd[:, which], nt_t[:, which])
                link(dve.scalar_tensor_tensor(out=nmr[:, which], in0=mv[:, which, :, 0], scalar=-1.0,
                                              in1=rstd[:, which], op0=ALU.mult, op1=ALU.mult))
                assert link.count[0] == LN_OPS

            def ln1(j):
                dve.wait_ge(xln_in, 16 * (j + 1))
                wait(dve, ln1_norm, 2 * j)
                ln_stats(chain(dve, ln1_chain, LN_OPS * j), x_ln, 0)

            def ln2(j):
                wait(dve, y2_done, 2 * j)
                ln_stats(chain(dve, ln2_chain, LN_OPS * j), x_res, 1)
                cols = bass.ds(2 * j, 2)
                dve.tensor_copy(ln2_r[:, cols], rstd[:, 1])
                dve.tensor_copy(ln2_b[:, cols], nmr[:, 1]).then_inc(ln2_stats, 1)

            def y_max(j, s):
                dve.wait_ge(y2_done, 2 * j + s + 1)
                dve.tensor_reduce(ymax[:, bass.ds(2 * j + s, 1)], y2[:], AX_X, ALU.max,
                                  apply_absolute_value=True).then_inc(ymax_done, 1)

            def residual(j, s):
                dve.wait_ge(o_mm, 2 * j + s + 1)
                if s == 0:
                    dve.wait_ge(xres_b, 2 * (j + 1))
                dve.tensor_tensor(x_res[:, s], (p3, p4)[s][:], x_res[:, s], ALU.add).then_inc(res_done, 1)

            def row_maxima(b, h):
                dve.wait_ge(s_mm, H * b + h + 1)
                apart(dve)
                for qb in range(2):
                    sc = ring[h % 3][:, qb * S:(qb + 1) * S]
                    dve.tensor_tensor_reduce(sc, sc, mask[:, qb], 1.0, NEG, ALU.add, ALU.max,
                                             row_max[:, qb, h:h + 1]).then_inc(max_done, 1)

            def split_max(b):
                dve.wait_ge(max_done, 2 * H * (b + 1))
                for qb in range(2):
                    m = row_max[:, qb:qb + 1].to_broadcast([P, ROWT, H])
                    dve.tensor_scalar(neg_max[:, qb, :, 0:H].bitcast(F32R), m, -1.0, None, ALU.mult).then_inc(msplit, 1)
                dve.wait_ge(msplit, 4 * b + 2)
                for qb in range(2):
                    m = row_max[:, qb:qb + 1].to_broadcast([P, ROWT, H])
                    dve.scalar_tensor_tensor(out=neg_max[:, qb, :, H:2 * H].bitcast(F32R), in0=m, scalar=-1.0,
                                             in1=neg_max[:, qb, :, 0:H], op0=ALU.mult, op1=ALU.subtract).then_inc(msplit, 1)

            def rotate(j, which):
                base = ROPE_OPS * j
                lo, hi = {"q": (p4, p5), "k": (p3, p4)}[which]
                cos, sin = (rope[:, 0], rope[:, 1]) if which == "q" else (rope[:, 2], rope[:, 3])
                dst = roped[:, 0 if which == "q" else 1]
                a, b = (z[:].rearrange("p (c s) -> p c s", c=2) for z in (lo, hi))
                dve.wait_ge(q_mm if which == "q" else k_mm, 2 * (j + 1))
                wait(dve, hi_done[which], j)
                wait(dve, lo_done[which], 2 * j)
                s = rope_step[which]
                dve.tensor_tensor(rt[:, 0], a, cos, ALU.mult).then_inc(s, 1)
                dve.tensor_tensor(rt[:, 1], b, sin, ALU.mult).then_inc(s, 1)
                dve.wait_ge(s, base + 2)
                dve.tensor_tensor(dst[:, 0:2], rt[:, 0], rt[:, 1], ALU.subtract).then_inc(s, 1)
                dve.wait_ge(s, base + 3)
                dve.tensor_tensor(rt[:, 0], a, sin, ALU.mult).then_inc(s, 1)
                dve.tensor_tensor(rt[:, 1], b, cos, ALU.mult).then_inc(s, 1)
                dve.wait_ge(s, base + 5)
                dve.tensor_tensor(dst[:, 2:4], rt[:, 0], rt[:, 1], ALU.add).then_inc(s, 1)
                dve.wait_ge(s, base + 6)

            def xt_rest(j, s):
                tok = slice(s * P, (s + 1) * P)
                dve.wait_ge(xt_hi, 2 * j + s + 1)
                dve.tensor_tensor(xT_lo[:, :, tok], (p3, p4)[s][:].rearrange("p (c t) -> p c t", c=KC),
                                  xT_hi[:, :, tok].bitcast(F32), ALU.subtract).then_inc(xt_lo, 1)

            def normalise(b, c):
                src = pv_bank[c % 2]
                dve.wait_ge(pv_mm, H * b + NC4 * (c + 1))
                wait(dve, onorm, KC * b + c)
                dve.reciprocal(o_rec[:], src[:, S:2 * S]).then_inc(rec_done, 1)
                dve.wait_ge(rec_done, KC * b + c + 1)
                wait(dve, ohi_done, KC * b + c)
                wait(dve, olo_done, KC * b + c)
                dve.tensor_tensor(o_f[:], src[:, 0:S], o_rec[:], ALU.mult).then_inc(onorm, 1)

            def quantise_win(b):
                dve.wait_ge(win_in, 16 * (b + 1))
                wait(dve, wt_mm, b)
                link = chain(dve, wq_chain, WQ_OPS * b)
                link(dve.tensor_reduce(w_s[:, 0:1], w_raw[:], AX_X, ALU.max, apply_absolute_value=True))
                link(dve.tensor_scalar(w_s[:, 1:2], w_s[:, 0:1], QMIN, None, ALU.max))
                link(dve.reciprocal(w_s[:, 2:3], w_s[:, 1:2]))
                link(dve.tensor_scalar(w_s[:, 3:4], w_s[:, 2:3], 127.0, None, ALU.mult))
                link(dve.tensor_scalar(w_raw[:], w_raw[:], w_s[:, 3:4], MAGIC, ALU.mult, ALU.add))
                link(dve.tensor_copy(win_amax[:, bass.ds(b, 1)], w_s[:, 1:2]))
                link(dve.tensor_scalar(w_q[:], w_raw[:], MAGIC, None, ALU.subtract))
                assert link.count[0] == WQ_OPS

            dve.memset(ones[:], 1.0).then_inc(ones_done, 1)
            dve.memset(magic_c[:], MAGIC).then_inc(ones_done, 1)
            ln1(0)
            dve.wait_ge(c_in, 16 * 5)
            dve.tensor_copy(ident_b[:], ident[:]).then_inc(ones_done, 1)
            stage = {"wv": v_sb[:].rearrange("p a b d -> p (a b) d"), "wk": v_sb[:].rearrange("p a b d -> p (a b) d"),
                     "wq": roped[:].rearrange("p a c s -> p (a c s)").rearrange("p (c e) -> p c e", c=KC),
                     "wo": roped[:].rearrange("p a c s -> p (a c s)").rearrange("p (c e) -> p c e", c=KC)}
            for i, n in enumerate(("wv", "wq", "wk", "wo")):
                dve.wait_ge(w_hi_done, i + 1)
                dve.tensor_tensor(w_lo[n][:], stage[n], w_hi[n][:].bitcast(F32), ALU.subtract).then_inc(w_lo_done, 1)
            xt_rest(0, 0)
            xt_rest(0, 1)
            dve.wait_ge(w_lo_done, 4)
            rotate(0, "q")
            rotate(0, "k")
            ln1(1)
            xt_rest(1, 0)
            xt_rest(1, 1)

            def step(b, par, has_o, has_proj, has_xt):
                for h in range(H):
                    row_maxima(b, h)
                    if has_o:
                        if h == 5:
                            residual(b - 1, 0)
                        if h == 7:
                            residual(b - 1, 1)
                            dve.wait_ge(res_done, 2 * b)
                            ln2(b - 1)
                        if h in (11, 13):
                            y_max(b - 1, (h - 11) // 2)
                    if h == 12:
                        quantise_win(b)
                split_max(b)
                if has_proj:
                    rotate(b + 1, "q")
                    rotate(b + 1, "k")
                if has_xt:
                    ln1(b + 2)
                normalise(b, 0)
                normalise(b, 1)
                if has_xt:
                    xt_rest(b + 2, 0)
                    xt_rest(b + 2, 1)
                normalise(b, 2)
                normalise(b, 3)

            steps(dve, step)
            residual(NB - 1, 0)
            residual(NB - 1, 1)
            dve.wait_ge(res_done, 2 * NB)
            ln2(NB - 1)
            y_max(NB - 1, 0)
            y_max(NB - 1, 1)
            dve.wait_ge(ymax_done, 2 * NB)
            dve.wait_ge(ln2_stats, NB)
            dve.drain().then_inc(a_done, 1)
            dve.wait_ge(a_done, 4)

            dve.tensor_reduce(tiny[:, 0:1], ymax[:], AX_X, ALU.max).then_inc(bset, 1)
            dve.wait_ge(bset_pool, 1)
            link = chain(dve, bset, 1)
            link(dve.tensor_scalar(tiny[:, 2:3], tiny[:, 1:2], QMIN, None, ALU.max))
            link(dve.reciprocal(tiny[:, 3:4], tiny[:, 2:3]))
            link(dve.tensor_scalar(tiny[:, 4:5], tiny[:, 3:4], 32767.0, None, ALU.mult))
            link(dve.tensor_scalar(x_a[:], ln2_r[:], tiny[:, 4:5], None, ALU.mult))
            link(dve.tensor_scalar(x_b[:], ln2_b[:], tiny[:, 4:5], None, ALU.mult))
            link(dve.tensor_scalar(tiny[:, 6:7], tiny[:, 2:3], 1.0 / 32767.0, 1.0 / 127.0, ALU.mult, ALU.mult))
            dve.tensor_scalar(g_scale[:], win_amax[:], tiny[:, 6:7], None, ALU.mult).then_inc(bset, 1)

            def round_tile(n, par):
                for u in range(SUB):
                    dve.wait_ge(z_done, SUB * n + u + 1)
                    dve.tensor_scalar(xq[:, par, u], xq[:, par, u], MAGIC, MAGIC, ALU.add, ALU.subtract).then_inc(z_round, 1)

            def rest(n, par):
                for c in range(KC):
                    dve.wait_ge(qt_hi, KC * n + c + 1)
                    dve.tensor_tensor(qT_lo[:, par, c], bank[4 + c][:], qT_hi[:, par, c], ALU.subtract).then_inc(qt_lo, 1)

            def quantise_wout(j, par):
                link = chain(dve, wo_chain, WO_OPS * j)
                col = bass.ds(j, 1)
                s = wp_s[:, par]
                dve.wait_ge(wo_raw_in[par], 8 * j + (16 if par == 0 else 8))
                link(dve.tensor_reduce(s[:, 0:1], wo_raw[:, par], AX_X, ALU.max, apply_absolute_value=True))
                link(dve.tensor_scalar(s[:, 1:2], s[:, 0:1], QMIN, None, ALU.max))
                link(dve.reciprocal(s[:, 2:3], s[:, 1:2]))
                link(dve.tensor_scalar(s[:, 3:4], s[:, 2:3], 127.0, None, ALU.mult))
                link(dve.tensor_scalar(wout_amax[:, col], s[:, 1:2], 1.0 / 127.0, None, ALU.mult))
                link(dve.tensor_scalar(wout_pow[:, col].bitcast(I32), wout_amax[:, col].bitcast(I32), 0x7F800000, None, ALU.bitwise_and))
                link(dve.tensor_scalar(wo_raw[:, par], wo_raw[:, par], s[:, 3:4], MAGIC, ALU.mult, ALU.add))
                link(dve.tensor_scalar(wout_int[:, bass.ds(j, 1)].rearrange("p o d -> p (o d)"), wo_raw[:, par], MAGIC,
                                       wout_pow[:, col], ALU.subtract, ALU.mult))
                assert link.count[0] == WO_OPS

            def tile_b(n, par, spilt, more):
                for f in range(FC):
                    dve.wait_ge(gelu_done, FC * n + f + 1)
                    src = h_ring[:, f % 4] if spilt else h_kept[:, (n - SPILT) * FC + f]
                    dve.tensor_reduce(hmax[:, bass.ds(FC * n + f, 1)], src, AX_X, ALU.max,
                                      apply_absolute_value=True).then_inc(hmax_done, 1)
                    if f == 5 and more:
                        round_tile(n + 1, 1 - par)
                    if f == 7:
                        quantise_wout(2 * n, 0)
                    if f == 11 and more:
                        rest(n + 1, 1 - par)
                    if f == 14:
                        quantise_wout(2 * n + 1, 1)

            round_tile(0, 0)
            rest(0, 0)
            tile_b(0, 0, True, True)
            tile_b(1, 1, True, True)
            with dve.Fori(1, SPILT // 2) as i:
                tile_b(2 * i, 0, True, True)
                tile_b(2 * i + 1, 1, True, True)
            for n in range(SPILT, NT):
                tile_b(n, n % 2, False, n + 1 < NT)

            dve.wait_ge(hmax_done, FC * NT)
            dve.tensor_reduce(tiny[:, 0:1], hmax[:], AX_X, ALU.max).then_inc(cset, 1)
            dve.wait_ge(cset_pool, 1)
            link = chain(dve, cset, 1)
            link(dve.tensor_scalar(tiny[:, 2:3], tiny[:, 1:2], QMIN, None, ALU.max))
            link(dve.reciprocal(tiny[:, 3:4], tiny[:, 2:3]))
            link(dve.tensor_scalar(tiny[:, 5:6], tiny[:, 3:4], 32767.0, None, ALU.mult))
            link(dve.tensor_scalar(tiny[:, 6:7], tiny[:, 2:3], 2.0 / 32767.0, None, ALU.mult))
            link(dve.tensor_scalar(wout_man[:].bitcast(I32), wout_amax[:].bitcast(I32), 0x007FFFFF, 0x3F800000,
                                   ALU.bitwise_and, ALU.bitwise_or))
            link(dve.tensor_scalar(wout_man[:], wout_man[:], 0.5, None, ALU.mult))

            def integers(i, f):
                dve.wait_ge(hint_done, FC * i + f + 1)
                dve.tensor_scalar(h_int[:, f % 4], h_int[:, f % 4], MAGIC, wout_man[:, f:f + 1],
                                  ALU.subtract, ALU.mult).then_inc(g_done, 1)

            def result(i, par):
                dve.wait_ge(y_mm, FC * (i + 1))
                dve.wait_ge(xc_b, SUB * (i + 1))
                for u in range(SUB):
                    if u < 2:
                        wait(dve, y_out[u], 32 * i)
                    else:
                        dve.wait_ge(y_out[u % 2], 32 * i + 16)
                    dve.scalar_tensor_tensor(out=o_out[:, u % 2], in0=bank[4 * par + u][:], scalar=tiny[:, 6:7],
                                             in1=xq[:, par, u], op0=ALU.mult, op1=ALU.add).then_inc(y_done, 1)

            def tile_c(i, par, has_last):
                for f in range(FC):
                    integers(i, f)
                    dve.wait_ge(ghi_done, FC * i + f + 1)
                    dve.tensor_tensor(g_lo[:, f % 4], h_int[:, f % 4], g_hi[:, f % 4], ALU.subtract).then_inc(glo_done, 1)
                    if f == 4 and has_last:
                        result(i - 1, 1 - par)

            tile_c(0, 0, False)
            tile_c(1, 1, True)
            with dve.Fori(1, NT // 2) as i:
                tile_c(2 * i, 0, True)
                tile_c(2 * i + 1, 1, True)
            result(NT - 1, 1)

        @block.gpsimd
        def _(pool):
            def split_lo(which, j, par, half):
                src, hi, lo = (0, q_hi, q_lo) if which == "q" else (1, k_hi, k_lo)
                c = slice(2 * half, 2 * half + 2)
                if half == 0:
                    pool.wait_ge(hi_done[which], j + 1)
                pool.tensor_tensor(lo[:, par, c], roped[:, src, c], hi[:, par, c].bitcast(F32), ALU.subtract).then_inc(lo_done[which], 1)

            def ctx_lo(j):
                pool.wait_ge(c_hi, j + 1)
                pool.tensor_tensor(cT_lo[:], ctx_raw[:], cT_hi[:].bitcast(F32), ALU.subtract).then_inc(c_lo, 1)

            def out_lo(b, c):
                pool.wait_ge(ohi_done, KC * b + c + 1)
                pool.tensor_tensor(o_lo[:, c], o_f[:], o_hi[:, c].bitcast(F32), ALU.subtract).then_inc(olo_done, 1)

            def bias_x(j):
                pool.wait_ge(xres_in, 16 * (j + 1))
                for s in range(2):
                    pool.tensor_tensor(x_res[:, s], x_res[:, s], wo_b[:], ALU.add).then_inc(xres_b, 1)

            def band(b, h):
                pool.wait_ge(exp_done, H * b + h + 1)
                apart(pool)
                lower, upper = probs[:, h % 4, 0, P:2 * P], probs[:, h % 4, 1, 0:P]
                pool.affine_select(out=lower, in_=lower, compare_op=ALU.is_ge, fill=0.0, base=0,
                                   pattern=[[-1, P]], channel_multiplier=1).then_inc(p_ready, 1)
                pool.affine_select(out=upper, in_=upper, compare_op=ALU.is_ge, fill=0.0, base=0,
                                   pattern=[[1, P]], channel_multiplier=-1).then_inc(p_ready, 1)

            pool.dma_start(sel[:], t["c_sel"]).then_inc(sel_in, 16)
            ctx_lo(0)
            for which in ("q", "k"):
                for half in range(2):
                    split_lo(which, 0, 0, half)
            ctx_lo(1)
            pool.wait_ge(c_in, 16 * 5)
            bias_x(0)
            pool.wait_ge(sel_in, 16)

            def step(b, par, has_o, has_proj, has_xt):
                for h in range(H):
                    band(b, h)
                    if has_proj:
                        if h in (3, 5):
                            split_lo("q", b + 1, 1 - par, (h - 3) // 2)
                        if h in (7, 8):
                            split_lo("k", b + 1, 1 - par, h - 7)
                    if h in (10, 14):
                        out_lo(b, (h - 10) // 4)
                if has_o:
                    bias_x(b)
                if has_xt:
                    ctx_lo(b + 2)
                out_lo(b, 2)
                out_lo(b, 3)

            steps(pool, step)
            pool.drain().then_inc(a_done, 1)
            pool.wait_ge(a_done, 4)

            pool.wait_ge(bset, 1)
            pool.partition_all_reduce(tiny[:, 1:2], tiny[:, 0:1], P, ABSMAX).then_inc(bset_pool, 1)
            pool.wait_ge(cset, 1)
            pool.partition_all_reduce(tiny[:, 1:2], tiny[:, 0:1], P, ABSMAX).then_inc(cset_pool, 1)
            pool.wait_ge(b_out_in, 16)

            def bias_tile(i, par):
                pool.wait_ge(xc_in[par], 8 * i + (16 if par == 0 else 8))
                for u in range(SUB):
                    pool.tensor_tensor(xq[:, par, u], xq[:, par, u], b_out[:], ALU.add).then_inc(xc_b, 1)

            with pool.Fori(0, NT // 2) as i:
                bias_tile(2 * i, 0)
                bias_tile(2 * i + 1, 1)


_WEIGHTS = {"wq": "L0_xattn_wq", "wk": "L0_xattn_wk", "wv": "L0_xattn_wv", "wo": "L0_xattn_wo_w"}


def kernel(**inputs):
    import concourse.bacc as _bacc
    from concourse.bass_utils import run_bass_kernel_spmd as _run

    a = {k: np.asarray(v) for k, v in inputs.items()}
    arrays = {"x": a["x"].reshape(TOK, D), "ctxT": a["ctx_1024"].reshape(TOK, D).T}
    for n, full in _WEIGHTS.items():
        arrays[n] = a[full].T
    arrays["wo_b"] = np.tile(a["L0_xattn_wo_b"], (P, 1))
    arrays["winT"] = a["L0_ffn_W_in"].T
    arrays["b_in"] = a["L0_ffn_b_in"].reshape(FC, P).T
    arrays["wout"] = a["L0_ffn_W_out"]
    arrays["b_out"] = np.tile(a["L0_ffn_b_out"], (P, 1))
    arrays.update(constants())
    arrays = {n: np.ascontiguousarray(v) for n, v in arrays.items()}

    nc = _bacc.Bacc("TRN2", target_bir_lowering=False, num_devices=1)
    t = {n: nc.dram_tensor("in_" + n, v.shape, mybir.dt.from_np(v.dtype), kind="ExternalInput").ap()
         for n, v in arrays.items()}
    t["out"] = nc.dram_tensor("out_0", (TOK, D), F32, kind="ExternalOutput").ap()
    build(nc, t)
    r = _run(nc, [{"in_" + n: v for n, v in arrays.items()}], core_ids=[0])
    return r.results[0]["out_0"].reshape(NB, S, D)
```

```python
from contextlib import ExitStack

import numpy as np

import concourse.bass as bass
from concourse import mybir

ACT = mybir.ActivationFunctionType
ALU = mybir.AluOpType
AX_X = mybir.AxisListType.X
F32 = mybir.dt.float32
F32R = mybir.dt.float32r
BF16 = mybir.dt.bfloat16
F16 = mybir.dt.float16
I32 = mybir.dt.int32
ABSMAX = bass.bass_isa.ReduceOp.absmax

P = 128
NB, S, D = 16, 256, 512
H, DK = 16, 32
FF = 2048
TOK = NB * S
KC = D // P
NC4 = H // KC
WINDOW = 128
STACK = P // DK
MROW = 3 * DK
VW = DK + 1
GW = NC4 * VW
FC = FF // P
TT = 512
NT = TOK // TT
SUB = TT // P
KEPT = 2
SPILT = NT - KEPT
EPS = 1e-5
SCORE_SCALE = float(np.sqrt(DK))
CONSTS = 3
TABLES = 5
QMIN = 1e-8
MAGIC = 1.5 * 2.0 ** 23
NEG = float(np.finfo(np.float32).min)
RSQRT_SEED = float(0x5F3759DF)
LN_ST = 7
LN_SC = 14


def constants():
    half = D // 2
    inv = (1.0 / np.float32(10000.0) ** (np.arange(half, dtype=np.float32) / np.float32(half))).astype(np.float32)
    ang = np.arange(S, dtype=np.float32)[None, :] * inv[:, None]
    cos, sin = np.cos(ang).astype(np.float32), np.sin(ang).astype(np.float32)
    lay = lambda a: np.ascontiguousarray(a.reshape(2, P, S).transpose(1, 0, 2).reshape(P, 2 * S).astype(np.float32))
    rope = np.stack([lay(cos), lay(sin)], 1)
    q, k = np.arange(S)[:, None], np.arange(S)[None, :]
    mask = np.where(np.abs(q - k) <= WINDOW, 0.0, NEG).astype(np.float32)
    mask = np.ascontiguousarray(mask.reshape(2, P, S).transpose(1, 0, 2))
    sel = np.zeros((P, H), np.float32)
    for h in range(H):
        sel[MROW + h, h] = sel[MROW + H + h, h] = 1.0
    return {"c_rope": rope, "c_mask": mask, "c_sel": sel, "c_ident": np.eye(P, dtype=np.float32)}


def build(nc, t):
    x_d, ctx_d, out_d = t["x"], t["ctxT"], t["out"]
    x_rows = x_d.rearrange("(n s p) d -> n p s d", p=P, s=2)
    ctx_cols = ctx_d.rearrange("(c p) t -> p c t", p=P)
    x1_d = nc.dram_tensor("x1_scratch", [TOK, D], F32, kind="Internal").ap()
    x1_rows = x1_d.rearrange("(n s p) d -> n p s d", p=P, s=2)
    x1_tiles = x1_d.rearrange("(n u p) d -> n p u d", p=P, u=SUB)
    out_tiles = out_d.rearrange("(n u p) d -> n p u d", p=P, u=SUB)
    hid_d = nc.dram_tensor("hidden_scratch", [SPILT * FC, P, TT], F32, kind="Internal").ap()
    win_rows = t["winT"].rearrange("(j p) d -> j p d", p=P)
    wout_rows = t["wout"].rearrange("(j p) d -> j p d", p=P)

    with ExitStack() as ctx:
        def sem(name):
            return ctx.enter_context(nc.semaphore(name))

        def sb(name, shape, dt=F32, where=ctx):
            return where.enter_context(nc.sbuf_tensor(name, shape, dt))

        win_int = sb("win_int", [P, KC, FF], BF16)
        ident = sb("ident", [P, P])
        ident_b = sb("ident_b", [P, P], BF16)
        ln2_r = sb("ln2_r", [P, 2 * NB])
        ln2_b = sb("ln2_b", [P, 2 * NB])
        ymax = sb("ymax", [P, 2 * NB])
        win_amax = sb("win_amax", [P, FC])
        b_in = sb("b_in", [P, FC])
        tiny = sb("tiny", [P, 8])
        magic_c = sb("magic_c", [P, 1])
        ln2_mv = sb("ln2_mv", [P, 2 * NB, 2])

        pa = ExitStack()
        w_hi, w_lo = {}, {}
        for n in ("wk", "wq", "wv", "wo"):
            w_hi[n] = sb(n + "_hi", [P, KC, D], F32R, pa)
            w_lo[n] = sb(n + "_lo", [P, KC, D], F32R, pa)
        rope = sb("rope", [P, 2, 2, S], F32, pa)
        mask = sb("mask", [P, 2, S], F32, pa)
        sel = sb("sel", [P, H], F32, pa)
        wo_b = sb("wo_b", [P, D], F32, pa)
        q_st = sb("q_st", [P, H, S], F32R, pa)
        k_st = sb("k_st", [P, H, S], F32R, pa)
        stage = sb("stage", [P, 2, KC, S], F32, pa)
        part_hi = {n: sb(n + "_hi", [P, KC, S], F32R, pa) for n in ("q", "k")}
        part_lo = {n: sb(n + "_lo", [P, KC, S], F32R, pa) for n in ("q", "k")}
        v_sb = sb("v_sb", [P, 2, 2, H, VW], F32, pa)
        probs = sb("probs", [P, 4, 2, S], F32, pa)
        t_hi = sb("t_hi", [P, KC, S], F32R, pa)
        t_lo = sb("t_lo", [P, KC, S], F32R, pa)
        ctx_raw = sb("ctx_raw", [P, KC, S], F32, pa)
        cT_hi = sb("cT_hi", [P, KC, S], F32R, pa)
        cT_lo = sb("cT_lo", [P, KC, S], F32R, pa)
        o_n = sb("o_n", [P, 2, KC, NC4, DK], F32, pa)
        o_rec = sb("o_rec", [P, 2, NC4, 1], F32, pa)
        x_ln = sb("x_ln", [P, 2, D], F32, pa)
        x_res = sb("x_res", [P, 2, D], F32, pa)
        rt = sb("rt", [P, 2, 2, S], F32, pa)
        roped = sb("roped", [P, KC, S], F32, pa)
        w_raw = sb("w_raw", [P, D], F32, pa)
        w_q = sb("w_q", [P, D], BF16, pa)
        row_max = sb("row_max", [P, 2, H], F32, pa)
        neg_max = sb("neg_max", [P, 2, P], F32, pa)
        bn = sb("bn", [P, 2, 2, 6], F32, pa)
        mv = sb("mv", [P, 2, 2, 2], F32, pa)
        veps = sb("veps", [P, 2], F32, pa)
        rstd = sb("rstd", [P, 2], F32, pa)
        nt_t = sb("nt_t", [P, 2], F32, pa)
        nmr = sb("nmr", [P, 2], F32, pa)
        veps2 = sb("veps2", [P, 2 * NB], F32, pa)
        nt_t2 = sb("nt_t2", [P, 2 * NB], F32, pa)
        dmax = sb("dmax", [P, 2 * NB], F32, pa)
        w_s = sb("w_s", [P, 4], F32, pa)
        pa.close()

        pb = ExitStack()
        wout_int = sb("wout_int", [P, FC, D], BF16, pb)
        h_kept = sb("h_kept", [P, KEPT * FC, TT], F32, pb)
        xq = sb("xq", [P, 2, SUB, D], F32, pb)
        qT_hi = sb("qT_hi", [P, 2, KC, TT], BF16, pb)
        qT_lo = sb("qT_lo", [P, 2, KC, TT], BF16, pb)
        h_ring = sb("h_ring", [P, 4, TT], F32, pb)
        wo_raw = sb("wo_raw", [P, 2, D], F32, pb)
        b_out = sb("b_out", [P, D], F32, pb)
        hmax = sb("hmax", [P, NT * FC], F32, pb)
        x_a = sb("x_a", [P, 2 * NB], F32, pb)
        x_b = sb("x_b", [P, 2 * NB], F32, pb)
        g_scale = sb("g_scale", [P, FC], F32, pb)
        wout_amax = sb("wout_amax", [P, FC], F32, pb)
        wout_pow = sb("wout_pow", [P, FC], F32, pb)
        wout_man = sb("wout_man", [P, FC], F32, pb)
        wp_s = sb("wp_s", [P, 2, 4], F32, pb)
        h_int = sb("h_int", [P, 4, TT], F32, pb)
        g_hi = sb("g_hi", [P, 4, TT], F16, pb)
        g_lo = sb("g_lo", [P, 4, TT], F16, pb)
        o_out = sb("o_out", [P, 2, D], F32, pb)
        pb.close()

        bank = [ctx.enter_context(nc.psum_tensor(f"bank{i}", [P, 512], F32)) for i in range(8)]
        ring = bank[0:2]
        kv_bank = bank[2:4]
        q_bank = bank[4:6]
        pv_bank = bank[6:8]

        c_in, ident_in, b_out_in = sem("c_in"), sem("ident_in"), sem("b_out_in")
        w_in = {n: sem("in_" + n) for n in ("wk", "wq", "wv", "wo")}
        w_hi_done, w_lo_done, const_done, sel_done = sem("w_hi_done"), sem("w_lo_done"), sem("const_done"), sem("sel_done")
        ones_done = sem("ones_done")
        ctx_in, xln_in, xres_in, win_in, x1_out = (sem(n) for n in ("ctx_in", "xln_in", "xres_in", "win_in", "x1_out"))
        ln1_moment, ln1_chain, ln1_norm = sem("ln1_moment"), sem("ln1_chain"), sem("ln1_norm")
        ln2_chain, y2_done, dmax_done, ln2_end = sem("ln2_chain"), sem("y2_done"), sem("dmax_done"), sem("ln2_end")
        xt_mm, xt_hi, xt_lo = sem("xt_mm"), sem("xt_hi"), sem("xt_lo")
        ot_mm, ot_hi, ot_lo = sem("ot_mm"), sem("ot_hi"), sem("ot_lo")
        c_hi, c_lo = sem("c_hi"), sem("c_lo")
        v_mm, o_mm, v_done = sem("v_mm"), sem("o_mm"), sem("v_done")
        qk_mm = {n: sem(n + "_mm") for n in ("q", "k")}
        rope_step = {n: sem(f"rope_{n}_step") for n in ("q", "k")}
        hi_done = {n: sem(n + "_hi_done") for n in ("q", "k")}
        lo_done = {n: sem(n + "_lo_done") for n in ("q", "k")}
        stage_in = {n: sem(n + "_stage_in") for n in ("q", "k")}
        stacked = {n: sem(n + "_stacked") for n in ("q", "k")}
        s_mm, max_done, msplit, mT_mm, mT_done = (sem(n) for n in ("s_mm", "max_done", "msplit", "mT_mm", "mT_done"))
        st_mm, exp_done, p_ready, pv_mm = sem("st_mm"), sem("exp_done"), sem("p_ready"), sem("pv_mm")
        rec_done, onorm = sem("rec_done"), sem("onorm")
        xres_b, res_done = sem("xres_b"), sem("res_done")
        wq_chain, wq_round, wt_mm, wt_done = sem("wq_chain"), sem("wq_round"), sem("wt_mm"), sem("wt_done")
        a_done = sem("a_done")
        passed = sem("passed")

        b_in_sem = [sem(f"xq_in{i}") for i in range(2)]
        wo_raw_in = [sem(f"wo_raw_in{i}") for i in range(2)]
        bset, bset_pool = sem("bset"), sem("bset_pool")
        z_done, z_round, qt_mm, qt_hi, qt_lo = (sem(n) for n in ("z_done", "z_round", "qt_mm", "qt_hi", "qt_lo"))
        h_mm, gelu_done, hmax_done = sem("h_mm"), sem("gelu_done"), sem("hmax_done")
        h_out = [sem(f"h_out{i}") for i in range(4)]
        wo_chain = sem("wo_chain")
        cset, cset_pool = sem("cset"), sem("cset_pool")
        h_in = [sem(f"h_in{i}") for i in range(4)]
        xc_in = [sem(f"xc_in{i}") for i in range(2)]
        xc_b = sem("xc_b")
        hint_done, g_done, ghi_done, glo_done, y_mm, y_done = (
            sem(n) for n in ("hint_done", "g_done", "ghi_done", "glo_done", "y_mm", "y_done"))
        y_out = [sem(f"y_out{i}") for i in range(2)]

        ROPE_OPS = 6
        WQ_OPS = 5
        WO_OPS = 8
        LN2_OPS = 5
        STAGED = 16 * (STACK - 1)
        SLOT = {"k": 0, "q": 1}

        ORDER = [NC4 * c + i for i in range(NC4) for c in range(KC)]

        def steps(e, step):
            step(0, 0, False, False, True, True)
            step(1, 1, False, True, True, True)
            with e.Fori(1, NB // 2 - 1) as i:
                step(2 * i, 0, True, True, True, True)
                step(2 * i + 1, 1, True, True, True, True)
            step(NB - 2, 0, True, True, True, False)
            step(NB - 1, 1, True, True, False, False)

        def wait(e, s, value):
            if isinstance(value, int) and value <= 0:
                return
            e.wait_ge(s, value)

        def chain(e, s, base, separate=False):
            n = [0]

            def link(ins):
                n[0] += 1
                ins.then_inc(s, 1)
                e.wait_ge(s, base + n[0])
                if separate:
                    apart(e)
            link.count = n
            return link

        def rsqrt_seed(dve, link, v, r):
            link(dve.tensor_scalar(r.bitcast(I32), v.bitcast(I32), 1, None, ALU.logical_shift_right))
            link(dve.tensor_scalar(r.bitcast(I32), r.bitcast(I32), -1.0, RSQRT_SEED, ALU.mult, ALU.add))

        def rsqrt(e, link, v, r, tmp):
            for _ in range(3):
                link(e.tensor_tensor(tmp, r, r, ALU.mult))
                link(e.tensor_tensor(tmp, tmp, v, ALU.mult))
                link(e.tensor_scalar(tmp, tmp, -0.5, 1.5, ALU.mult, ALU.add))
                link(e.tensor_tensor(r, r, tmp, ALU.mult))

        def apart(e):
            e.sem_inc(passed, 1)

        v_flat = v_sb[:].rearrange("p a b h e -> p (a b h e)")[:, 0:KC * D]
        weight_stage = {"wk": v_flat.rearrange("p (c e) -> p c e", c=KC),
                        "wq": probs[:].rearrange("p a k q -> p a (k q)"),
                        "wv": stage[:].rearrange("p n (c a) t -> p (n c) (a t)", c=2),
                        "wo": probs[:].rearrange("p a k q -> p a (k q)")}

        block = ctx.enter_context(nc.Block())

        @block.sync
        def _(sp):
            def load_ctx(j):
                wait(sp, c_lo, 2 * j)
                sp.dma_start(ctx_raw[:], ctx_cols[:, :, bass.ds(j * S, S)]).then_inc(ctx_in, 16)

            def load_xln(j):
                wait(sp, xt_mm, 2 * j)
                sp.dma_start(x_ln[:], x_rows[bass.ds(j, 1)].rearrange("o p s d -> p (o s) d")).then_inc(xln_in, 16)

            def load_xres(j):
                wait(sp, x1_out, 16 * j)
                apart(sp)
                wait(sp, y2_done, 2 * j)
                sp.dma_start(x_res[:], x_rows[bass.ds(j, 1)].rearrange("o p s d -> p (o s) d")).then_inc(xres_in, 16)

            def store_x1(j):
                sp.wait_ge(res_done, 2 * j + 2)
                sp.dma_start(x1_rows[bass.ds(j, 1)].rearrange("o p s d -> p (o s) d"), x_res[:]).then_inc(x1_out, 16)

            def load_win(j):
                wait(sp, wq_round, 2 * j)
                sp.dma_start(w_raw[:], win_rows[bass.ds(j, 1)].rearrange("o p d -> p (o d)")).then_inc(win_in, 16)

            def stage_group(n, j, i):
                rows = slice(DK * i, DK * (i + 1))
                if i == 0:
                    sp.wait_ge(lo_done[n], 2 * (j + 1))
                    apart(sp)
                wait(sp, stacked[n], NC4 * j + i)
                for r, part in enumerate({"k": (part_hi, part_lo, part_hi), "q": (part_hi, part_hi, part_lo)}[n]):
                    sp.dma_start(stage[DK * r:DK * (r + 1), SLOT[n]], part[n][rows].bitcast(F32)).then_inc(stage_in[n], 16)

            wsrc = {n: t[n].rearrange("(c p) e -> p c e", p=P) for n in ("wk", "wq", "wv", "wo")}
            load_xln(0)
            sp.dma_start(ident[:], t["c_ident"]).then_inc(ident_in, 16)
            load_ctx(0)
            for n in ("wk", "wq", "wv"):
                sp.dma_start(weight_stage[n], wsrc[n]).then_inc(w_in[n], 16)
            sp.dma_start(rope[:].rearrange("p a b s -> p a (b s)"), t["c_rope"]).then_inc(c_in, 16)
            sp.dma_start(mask[:], t["c_mask"]).then_inc(c_in, 16)
            sp.dma_start(sel[:], t["c_sel"]).then_inc(c_in, 16)
            sp.dma_start(wo_b[:], t["wo_b"]).then_inc(c_in, 16)
            sp.dma_start(b_in[:], t["b_in"]).then_inc(c_in, 16)
            load_xln(1)
            load_ctx(1)
            load_win(0)
            sp.wait_ge(w_lo_done, 2)
            sp.dma_start(weight_stage["wo"], wsrc["wo"]).then_inc(w_in["wo"], 16)
            sp.wait_ge(w_lo_done, 3)
            stage_group("k", 0, 0)
            stage_group("q", 0, 0)
            stage_group("k", 0, 1)
            stage_group("q", 0, 1)
            load_ctx(2)
            stage_group("k", 0, 2)
            stage_group("k", 0, 3)

            def step(b, has_o, has_proj, has_xt, has_next):
                stage_group("q", b, 2)
                if has_o:
                    load_xres(b - 1)
                stage_group("q", b, 3)
                if has_xt:
                    load_xln(b + 2)
                if has_proj:
                    stage_group("k", b + 1, 0)
                    stage_group("k", b + 1, 1)
                    stage_group("q", b + 1, 0)
                    stage_group("k", b + 1, 2)
                if has_next:
                    load_ctx(b + 3)
                if has_proj:
                    stage_group("q", b + 1, 1)
                    stage_group("k", b + 1, 3)
                    load_win(b + 1)
                if has_o:
                    store_x1(b - 1)

            step(0, False, True, True, True)
            step(1, True, True, True, True)
            with sp.Fori(1, NB // 2 - 2) as i:
                step(2 * i, True, True, True, True)
                step(2 * i + 1, True, True, True, True)
            for b in range(NB - 4, NB):
                step(b, True, b + 1 < NB, b + 2 < NB, b + 3 < NB)
            load_xres(NB - 1)
            store_x1(NB - 1)
            sp.wait_ge(x1_out, 16 * NB)
            sp.wait_ge(a_done, 4)
            sp.dma_start(b_out[:], t["b_out"]).then_inc(b_out_in, 16)

            def load_xq(n, par):
                wait(sp, qt_mm, n - 1)
                sp.dma_start(xq[:, par], x1_tiles[bass.ds(n, 1)].rearrange("o p u d -> p (o u) d")).then_inc(b_in_sem[par], 16)

            def load_wout(j, par):
                wait(sp, wo_chain, WO_OPS * (j - 1))
                sp.dma_start(wo_raw[:, par], wout_rows[bass.ds(j, 1)].rearrange("o p d -> p (o d)")).then_inc(wo_raw_in[par], 16)

            def store_hidden(n):
                for f in range(FC):
                    sp.wait_ge(gelu_done, FC * n + f + 1)
                    sp.dma_start(hid_d[bass.ds(FC * n + f, 1)].rearrange("o p t -> p (o t)"), h_ring[:, f % 4]).then_inc(h_out[f % 4], 16)

            def tile_b(n, par, spilt, more):
                load_wout(2 * n, 0)
                load_wout(2 * n + 1, 1)
                if spilt:
                    store_hidden(n)
                if more:
                    load_xq(n + 2, par)

            load_xq(0, 0)
            load_xq(1, 1)
            tile_b(0, 0, True, True)
            tile_b(1, 1, True, True)
            with sp.Fori(1, SPILT // 2) as i:
                tile_b(2 * i, 0, True, True)
                tile_b(2 * i + 1, 1, True, True)
            for n in range(SPILT, NT):
                tile_b(n, n % 2, False, n + 2 < NT)

            def load_xc(i, par, tile):
                wait(sp, qt_mm, NT)
                wait(sp, y_done, SUB * (i - 1))
                sp.dma_start(xq[:, par], x1_tiles[bass.ds(tile, 1)].rearrange("o p u d -> p (o u) d")).then_inc(xc_in[par], 16)

            def store_y(i, tile):
                for u in range(SUB):
                    sp.wait_ge(y_done, SUB * i + u + 1)
                    sp.dma_start(out_tiles[bass.ds(tile, 1), :, u].rearrange("o p d -> p (o d)"), o_out[:, u % 2]).then_inc(y_out[u % 2], 16)

            load_xc(0, 0, SPILT)
            load_xc(1, 1, SPILT + 1)
            for i in range(KEPT):
                store_y(i, SPILT + i)
                load_xc(i + 2, i % 2, SPILT + i + 2 if i + 2 < KEPT else i + 2 - KEPT)
            for i in range(SPILT):
                store_y(KEPT + i, i)
                if i + 2 < SPILT:
                    load_xc(KEPT + i + 2, i % 2, i + 2)
            for q in y_out:
                sp.wait_ge(q, 16 * NT * SUB // 2)

        @block.tensor
        def _(pe):
            def split3(out, lhs, rhs, first, last):
                (l_hi, l_lo), (r_hi, r_lo) = lhs, rhs
                pe.matmul(out, l_hi, r_hi, start=first, stop=False)
                pe.matmul(out, l_hi, r_lo, start=False, stop=False)
                return pe.matmul(out, l_lo, r_hi, start=False, stop=last)

            def x_transposes(j, s):
                if s == 0:
                    pe.wait_ge(ln1_norm, 2 * j + 2)
                    wait(pe, wt_done, j - 1)
                    wait(pe, rope_step["q"], ROPE_OPS * j)
                for c in range(KC):
                    mm = pe.transpose(q_bank[s][:, c * P:(c + 1) * P], x_ln[:, s, c * P:(c + 1) * P], ident[:])
                mm.then_inc(xt_mm, 1)

            def o_transposes(j, s):
                if s == 0:
                    pe.wait_ge(onorm, NC4 * (j + 1))
                for c in range(KC):
                    mm = pe.transpose(pv_bank[s][:, c * P:(c + 1) * P], o_n[:, s, c].rearrange("p i d -> p (i d)"), ident[:])
                mm.then_inc(ot_mm, 1)

            def v_tile(j, s):
                pe.wait_ge(rope_step["k"], ROPE_OPS * (j + 1))
                for c in range(KC):
                    tok = slice(s * P, (s + 1) * P)
                    mm = split3(kv_bank[s][:], (cT_hi[:, c, tok], cT_lo[:, c, tok]),
                                (w_hi["wv"][:, c], w_lo["wv"][:, c]), c == 0, c == KC - 1)
                mm.then_inc(v_mm, 1)

            def qk_tile(j, which, half):
                src = (t_hi, t_lo) if which == "q" else (cT_hi, cT_lo)
                if which == "k":
                    if half == 0:
                        pe.wait_ge(c_hi, j + 1)
                        pe.wait_ge(c_lo, 2 * (j + 1))
                    wait(pe, res_done, 2 * (j - 2) + half - 1)
                elif half == 0:
                    pe.wait_ge(xt_hi, 2 * j + 2)
                    pe.wait_ge(xt_lo, 2 * j + 2)
                dst = (kv_bank if which == "k" else q_bank)[half]
                w = "w" + which
                for a in range(2):
                    e = slice((2 * half + a) * P, (2 * half + a + 1) * P)
                    for c in range(KC):
                        mm = split3(dst[:, a * S:(a + 1) * S], (w_hi[w][:, c, e], w_lo[w][:, c, e]),
                                    (src[0][:, c], src[1][:, c]), c == 0, c == KC - 1)
                mm.then_inc(qk_mm[which], 1)

            def o_products(j, has_proj):
                for s in range(2):
                    tok = slice(s * P, (s + 1) * P)
                    if s == 0:
                        pe.wait_ge(ot_hi, 2 * (j + 1))
                        pe.wait_ge(ot_lo, 2 * (j + 1))
                        pe.wait_ge(w_lo_done, 4)
                    if has_proj:
                        pe.wait_ge(v_done, 2 * (j + 2) + s + 1)
                    else:
                        pe.wait_ge(res_done, 2 * j)
                    for c in range(KC):
                        parts = ((t_hi, "hi"), (t_hi, "lo"), (t_lo, "hi"))
                        for m, (part, w) in enumerate(parts):
                            mm = pe.matmul(kv_bank[s][:], part[:, c, tok], (w_hi if w == "hi" else w_lo)["wo"][:, c],
                                           start=c == 0 and m == 0, stop=c == KC - 1 and m == 2)
                            if c == KC - 1 and m == 2:
                                mm.then_inc(o_mm, 1)
                            yield

            def scores(b, n):
                if n % KC == 0:
                    for name in ("k", "q"):
                        pe.wait_ge(stacked[name], NC4 * b + n // KC + 1)
                if n < 2:
                    wait(pe, exp_done, H * b)
                else:
                    pe.wait_ge(max_done, 2 * (H * b + n - 1))
                for qb in range(2):
                    mm = pe.matmul(ring[n % 2][:, qb * S:(qb + 1) * S], q_st[0:MROW, ORDER[n], qb * P:(qb + 1) * P],
                                   k_st[0:MROW, ORDER[n]], start=True, stop=True)
                mm.then_inc(s_mm, 1)

            def max_transposes(b):
                pe.wait_ge(msplit, 2 * (b + 1))
                wait(pe, ot_lo, 2 * b)
                for qb in range(2):
                    mm = pe.transpose(pv_bank[1][:, qb * P:(qb + 1) * P], neg_max[:, qb], ident[:])
                mm.then_inc(mT_mm, 1)

            def scores_t(b, n):
                if n % KC == 0:
                    pe.wait_ge(mT_done, NC4 * b + n // KC + 1)
                if n < 2:
                    pe.wait_ge(max_done, 2 * H * (b + 1))
                else:
                    pe.wait_ge(exp_done, H * b + n - 1)
                for kb in range(2):
                    mm = pe.matmul(ring[n % 2][:, kb * S:(kb + 1) * S], k_st[:, ORDER[n], kb * P:(kb + 1) * P],
                                   q_st[:, ORDER[n]], start=True, stop=True)
                mm.then_inc(st_mm, 1)

            def weighted(b, par, n):
                i, c = n // KC, n % KC
                pe.wait_ge(p_ready, 2 * (H * b + n + 1))
                if n == 0:
                    pe.wait_ge(v_done, 2 * (b + 1))
                    wait(pe, ot_lo, 2 * b - 1)
                elif n == KC:
                    pe.wait_ge(mT_done, NC4 * (b + 1))
                elif c == 0:
                    pe.wait_ge(onorm, NC4 * b + i - 1)
                for qb in range(2):
                    for kb in range(2):
                        mm = pe.matmul(pv_bank[i % 2][:, qb * GW + c * VW:qb * GW + (c + 1) * VW],
                                       probs[:, n % 4, kb, qb * P:(qb + 1) * P], v_sb[:, par, kb, ORDER[n]],
                                       start=kb == 0, stop=kb == 1)
                mm.then_inc(pv_mm, 1)

            def w_transposes(b, has_proj):
                pe.wait_ge(wq_round, 2 * (b + 1))
                if has_proj:
                    pe.wait_ge(rope_step["q"], ROPE_OPS * (b + 2))
                else:
                    pe.wait_ge(wt_done, b)
                dst = q_bank[0][:].bitcast(BF16)
                for c in range(KC):
                    mm = pe.transpose(dst[:, c * P:(c + 1) * P], w_q[:, c * P:(c + 1) * P], ident_b[:])
                mm.then_inc(wt_mm, 1)

            pe.wait_ge(ident_in, 16)
            pe.wait_ge(const_done, CONSTS)
            x_transposes(0, 0)
            x_transposes(0, 1)
            for i, which in enumerate(("k", "q")):
                pe.wait_ge(w_lo_done, i + 1)
                qk_tile(0, which, 0)
                qk_tile(0, which, 1)
            pe.wait_ge(w_lo_done, 3)
            v_tile(0, 0)
            v_tile(0, 1)
            pe.wait_ge(sel_done, 1)
            pe.wait_ge(ones_done, 1)

            LAG = 3

            def step(b, par, has_c, has_o, has_proj, has_xt):
                tiles = [[] for _ in range(H // 2)]
                if has_proj:
                    tiles[0] += [lambda: qk_tile(b + 1, "k", 0)]
                    tiles[1] += [lambda: qk_tile(b + 1, "k", 1), lambda: x_transposes(b + 1, 0), lambda: x_transposes(b + 1, 1)]
                if has_o:
                    tiles[2] += [lambda: o_transposes(b - 1, 0), lambda: o_transposes(b - 1, 1)]
                if has_proj:
                    tiles[3] += [lambda: qk_tile(b + 1, "q", 0)]
                    tiles[4] += [lambda: qk_tile(b + 1, "q", 1)]
                    tiles[6] += [lambda: v_tile(b + 1, 0)]
                    tiles[7] += [lambda: v_tile(b + 1, 1)]
                for n in range(H):
                    scores(b, n)
                    if n % 2:
                        for tile in tiles[n // 2]:
                            tile()
                max_transposes(b)
                heavy = o_products(b - 1, has_proj) if has_o else iter(())
                for _ in range(5):
                    next(heavy, None)
                for n in range(H + LAG):
                    if n < H:
                        scores_t(b, n)
                    for _ in range(1 + (n % 4 == 0)):
                        next(heavy, None)
                    if n >= LAG:
                        weighted(b, par, n - LAG)
                assert next(heavy, "none") == "none"
                w_transposes(b, has_proj)

            steps(pe, step)
            o_transposes(NB - 1, 0)
            o_transposes(NB - 1, 1)
            for _ in o_products(NB - 1, False):
                pass
            pe.wait_ge(res_done, 2 * NB)
            pe.drain().then_inc(a_done, 1)
            pe.wait_ge(a_done, 4)

            def q_transposes(n, par):
                for u in range(SUB):
                    pe.wait_ge(z_round, SUB * n + u + 1)
                    if u == 0:
                        wait(pe, qt_lo, KC * n)
                        wait(pe, qt_hi, KC * n)
                    for c in range(KC):
                        mm = pe.transpose(bank[4 + c][:, u * P:(u + 1) * P], xq[:, par, u, c * P:(c + 1) * P], ident[:])
                mm.then_inc(qt_mm, 1)

            def hidden_chunk(n, par, f):
                if f == 0:
                    pe.wait_ge(qt_hi, KC * (n + 1))
                    pe.wait_ge(qt_lo, KC * (n + 1))
                wait(pe, gelu_done, FC * n + f - 3)
                for c in range(KC):
                    for part in (qT_hi, qT_lo):
                        mm = pe.matmul(bank[f % 4][:], win_int[:, c, f * P:(f + 1) * P], part[:, par, c],
                                       start=c == 0 and part is qT_hi, stop=c == KC - 1 and part is qT_lo)
                mm.then_inc(h_mm, 1)

            def tile_b(n, par, more):
                for f in range(FC):
                    hidden_chunk(n, par, f)
                    if f == 9 and more:
                        q_transposes(n + 1, 1 - par)

            q_transposes(0, 0)
            tile_b(0, 0, True)
            tile_b(1, 1, True)
            with pe.Fori(1, SPILT // 2) as i:
                tile_b(2 * i, 0, True)
                tile_b(2 * i + 1, 1, True)
            for n in range(SPILT, NT):
                tile_b(n, n % 2, n + 1 < NT)

            pe.wait_ge(wo_chain, WO_OPS * FC)
            pe.wait_ge(gelu_done, FC * NT)

            def tile_c(i, par):
                wait(pe, y_done, SUB * (i - 1))
                for f in range(FC):
                    pe.wait_ge(ghi_done, FC * i + f + 1)
                    pe.wait_ge(glo_done, FC * i + f + 1)
                    for u in range(SUB):
                        for part in (g_hi, g_lo):
                            mm = pe.matmul(bank[4 * par + u][:], part[:, f % 4, u * P:(u + 1) * P], wout_int[:, f],
                                           start=f == 0 and part is g_hi, stop=f == FC - 1 and part is g_lo)
                    mm.then_inc(y_mm, 1)

            tile_c(0, 0)
            tile_c(1, 1)
            with pe.Fori(1, NT // 2) as i:
                tile_c(2 * i, 0)
                tile_c(2 * i + 1, 1)

        @block.scalar
        def _(act):
            def split_hi(which, j):
                act.wait_ge(rope_step[which], ROPE_OPS * (j + 1))
                wait(act, stage_in[which], STAGED * NC4 * j)
                act.copy(part_hi[which][:], roped[:]).then_inc(hi_done[which], 1)

            def ctx_hi(j):
                act.wait_ge(ctx_in, 16 * (j + 1))
                wait(act, v_mm, 2 * j)
                act.copy(cT_hi[:], ctx_raw[:]).then_inc(c_hi, 1)

            def norm1(j):
                act.wait_ge(ln1_chain, LN_SC * (j + 1))
                for s in range(2):
                    act.activation(x_ln[:, s], x_ln[:, s], ACT.Identity, bias=nmr[:, s:s + 1],
                                   scale=rstd[:, s:s + 1]).then_inc(ln1_norm, 1)

            def lead(src, s, done):
                act.copy(t_hi[:, :, s * P:(s + 1) * P], src[s][:].rearrange("p (c t) -> p c t", c=KC)).then_inc(done, 1)

            def xt_lead(j, s):
                act.wait_ge(xt_mm, 2 * j + s + 1)
                lead(q_bank, s, xt_hi)

            def ot_lead(j, s, has_q):
                act.wait_ge(ot_mm, 2 * j + s + 1)
                if s == 0 and has_q:
                    act.wait_ge(qk_mm["q"], 2 * (j + 3))
                lead(pv_bank, s, ot_hi)

            def v_copy(j, par, s):
                act.wait_ge(v_mm, 2 * j + s + 1)
                act.copy(v_sb[:, par, s, :, 0:DK], kv_bank[s][:].rearrange("p (h d) -> p h d", h=H)).then_inc(v_done, 1)

            def centre(j, s):
                if s == 0:
                    act.wait_ge(ln2_chain, LN2_OPS * (j + 1) - 1)
                    wait(act, dmax_done, 2 * j)
                act.activation(rt[:, s].rearrange("p c t -> p (c t)"), x_res[:, s], ACT.Identity, bias=mv[:, 1, s, 0:1], scale=-1.0).then_inc(y2_done, 1)

            def max_copy(b, i):
                act.wait_ge(mT_mm, b + 1)
                act.copy(q_st[MROW:P, i::NC4, :],
                         pv_bank[1][MROW:P, 0:S].rearrange("p (o t) -> p o t", o=1).to_broadcast([P - MROW, KC, S])).then_inc(mT_done, 1)

            def stack_q(j, i):
                act.wait_ge(stage_in["q"], STAGED * (NC4 * j + i + 1))
                wait(act, st_mm, H * (j - 1) + KC * (i + 1))
                act.copy(q_st[0:MROW, i::NC4, :], stage[0:MROW, SLOT["q"]]).then_inc(stacked["q"], 1)

            def softmax_exp(b, n):
                act.wait_ge(st_mm, H * b + n + 1)
                wait(act, pv_mm, H * b + n - 3)
                act.activation(probs[:, n % 4].rearrange("p k q -> p (k q)"), ring[n % 2][:], ACT.Exp,
                               scale=SCORE_SCALE).then_inc(exp_done, 1)

            act.wait_ge(xln_in, 16)
            norm1(0)
            ctx_hi(0)
            xt_lead(0, 0)
            xt_lead(0, 1)

            def weight_hi(n):
                act.wait_ge(w_in[n], 16)
                act.copy(w_hi[n][:], weight_stage[n]).then_inc(w_hi_done, 1)

            for n in ("wk", "wq", "wv"):
                weight_hi(n)
            split_hi("k", 0)
            split_hi("q", 0)
            weight_hi("wo")
            v_copy(0, 0, 0)
            v_copy(0, 0, 1)
            ctx_hi(1)
            stack_q(0, 0)
            stack_q(0, 1)

            def step(b, par, has_c, has_o, has_proj, has_xt):
                stack_q(b, 2)
                if has_c:
                    centre(b - 2, 0)
                    centre(b - 2, 1)
                if has_proj:
                    norm1(b + 1)
                stack_q(b, 3)
                if has_proj:
                    xt_lead(b + 1, 0)
                    xt_lead(b + 1, 1)
                    split_hi("k", b + 1)
                if has_o:
                    ot_lead(b - 1, 0, has_proj)
                    ot_lead(b - 1, 1, has_proj)
                if has_proj:
                    v_copy(b + 1, 1 - par, 0)
                    v_copy(b + 1, 1 - par, 1)
                max_copy(b, 0)
                for n in range(H):
                    softmax_exp(b, n)
                    if n in (1, 3, 5):
                        max_copy(b, (n + 1) // 2)
                    if n == 4 and has_proj:
                        split_hi("q", b + 1)
                    if n == 8 and has_xt:
                        ctx_hi(b + 2)
                    if n in (12, 14) and has_proj:
                        stack_q(b + 1, (n - 12) // 2)
                act.wait_ge(wt_mm, b + 1)
                act.copy(win_int[:, :, bass.ds(b * P, P)],
                         q_bank[0][:].bitcast(BF16)[:, 0:D].rearrange("p (c f) -> p c f", c=KC)).then_inc(wt_done, 1)

            steps(act, step)
            centre(NB - 2, 0)
            centre(NB - 2, 1)
            ot_lead(NB - 1, 0, False)
            ot_lead(NB - 1, 1, False)
            centre(NB - 1, 0)
            centre(NB - 1, 1)
            act.wait_ge(y2_done, 2 * NB)
            act.drain().then_inc(a_done, 1)
            act.wait_ge(a_done, 4)

            act.wait_ge(bset, 7)

            def scale_tile(n, par):
                act.wait_ge(b_in_sem[par], 8 * n + (16 if par == 0 else 8))
                for u in range(SUB):
                    col = bass.ds(SUB * n + u, 1)
                    act.activation(xq[:, par, u], xq[:, par, u], ACT.Identity, bias=x_b[:, col],
                                   scale=x_a[:, col]).then_inc(z_done, 1)

            def lead(n, par):
                act.wait_ge(qt_mm, n + 1)
                for c in range(KC):
                    act.copy(qT_hi[:, par, c], bank[4 + c][:]).then_inc(qt_hi, 1)

            def tile_b(n, par, spilt, more):
                for f in range(FC):
                    act.wait_ge(h_mm, FC * n + f + 1)
                    if spilt:
                        if f < 4:
                            wait(act, h_out[f], 64 * n)
                            wait(act, hmax_done, FC * n + f - 3)
                        else:
                            act.wait_ge(h_out[f % 4], 64 * n + 16 * (f // 4))
                            act.wait_ge(hmax_done, FC * n + f - 3)
                        dst = h_ring[:, f % 4]
                    else:
                        dst = h_kept[:, (n - SPILT) * FC + f]
                    act.activation(dst, bank[f % 4][:], ACT.Gelu, bias=b_in[:, f:f + 1],
                                   scale=g_scale[:, f:f + 1]).then_inc(gelu_done, 1)
                    if f == 4 and more:
                        scale_tile(n + 1, 1 - par)
                    if f == 11 and more:
                        lead(n + 1, 1 - par)

            scale_tile(0, 0)
            lead(0, 0)
            tile_b(0, 0, True, True)
            tile_b(1, 1, True, True)
            with act.Fori(1, SPILT // 2) as i:
                tile_b(2 * i, 0, True, True)
                tile_b(2 * i + 1, 1, True, True)
            for n in range(SPILT, NT):
                tile_b(n, n % 2, False, n + 1 < NT)

            act.wait_ge(cset, 4)

            def load_hidden(n, f):
                act.dma_start(h_ring[:, f % 4], hid_d[bass.ds(FC * n + f, 1)].rearrange("o p t -> p (o t)")).then_inc(h_in[f % 4], 16)

            for q in h_out:
                act.wait_ge(q, 16 * SPILT * FC // 4)
            for f in range(4):
                load_hidden(0, f)

            def lead_c(i, f):
                act.wait_ge(g_done, FC * i + f + 1)
                if f >= 4:
                    act.wait_ge(y_mm, FC * i + f - 3)
                else:
                    wait(act, y_mm, FC * i + f - 3)
                act.copy(g_hi[:, f % 4], h_int[:, f % 4]).then_inc(ghi_done, 1)

            def tile_c(i, src, spilt, more):
                for f in range(FC + 1):
                    if f < FC:
                        if spilt:
                            act.wait_ge(h_in[f % 4], 64 * src + 16 * (f // 4) + 16)
                        wait(act, glo_done, FC * i + f - 3)
                        wait(act, ghi_done, FC * i + f - 3)
                        chunk = h_ring[:, f % 4] if spilt else h_kept[:, FC * src + f]
                        act.activation(h_int[:, f % 4], chunk, ACT.Identity, bias=magic_c[:], scale=tiny[:, 5:6]).then_inc(hint_done, 1)
                    if f >= 1:
                        lead_c(i, f - 1)
                        if spilt and (more or f - 1 + 4 < FC):
                            act.wait_ge(hint_done, FC * i + f)
                            n, g = (src, f + 3) if f + 3 < FC else (src + 1, f + 3 - FC)
                            load_hidden(n, g)

            for i in range(KEPT):
                tile_c(i, i, False, True)
            with act.Fori(0, SPILT - 1) as i:
                tile_c(KEPT + i, i, True, True)
            tile_c(NT - 1, SPILT - 1, True, False)

        @block.vector
        def _(dve):
            def moments(link, src, which):
                for s in range(2):
                    link(dve.bn_stats(bn[:, which, s], src[:, s]))
                for s in range(2):
                    apart(dve)
                    link(dve.bn_aggr(mv[:, which, s], bn[:, which, s]))

            def ln1_moments(j):
                dve.wait_ge(xln_in, 16 * (j + 1))
                wait(dve, ln1_chain, LN_SC * j)
                link = chain(dve, ln1_moment, LN_ST * j)
                moments(link, x_ln, 0)
                wait(dve, ln1_norm, 2 * j)
                apart(dve)
                link(dve.tensor_scalar(veps[:], mv[:, 0, :, 1], EPS, None, ALU.add))
                rsqrt_seed(dve, link, veps[:], rstd[:])
                assert link.count[0] == LN_ST

            def ln2_moments(j):
                dve.wait_ge(res_done, 2 * (j + 1))
                wait(dve, y2_done, 2 * j)
                link = chain(dve, ln2_chain, LN2_OPS * j)
                moments(link, x_res, 1)
                link(dve.tensor_copy(ln2_mv[:, bass.ds(2 * j, 2)], mv[:, 1]))
                assert link.count[0] == LN2_OPS

            def largest(j, s):
                dve.wait_ge(y2_done, 2 * j + s + 1)
                dve.tensor_reduce(dmax[:, bass.ds(2 * j + s, 1)], rt[:, s].rearrange("p c t -> p (c t)"), AX_X, ALU.max,
                                  apply_absolute_value=True).then_inc(dmax_done, 1)

            def residual(j, s):
                dve.wait_ge(o_mm, 2 * j + s + 1)
                if s == 0:
                    dve.wait_ge(xres_b, 2 * (j + 1))
                dve.tensor_tensor(x_res[:, s], kv_bank[s][:], x_res[:, s], ALU.add).then_inc(res_done, 1)

            def row_maxima(b, n):
                h = ORDER[n]
                dve.wait_ge(s_mm, H * b + n + 1)
                apart(dve)
                for qb in range(2):
                    sc = ring[n % 2][:, qb * S:(qb + 1) * S]
                    dve.tensor_tensor_reduce(sc, sc, mask[:, qb], 1.0, NEG, ALU.add, ALU.max,
                                             row_max[:, qb, h:h + 1]).then_inc(max_done, 1)

            def split_max(b):
                dve.wait_ge(max_done, 2 * H * (b + 1))
                dve.tensor_scalar(neg_max[:, :, MROW:MROW + H].bitcast(F32R), row_max[:], -1.0, None, ALU.mult).then_inc(msplit, 1)
                dve.wait_ge(msplit, 2 * b + 1)
                dve.scalar_tensor_tensor(out=neg_max[:, :, MROW + H:P].bitcast(F32R), in0=row_max[:], scalar=-1.0,
                                         in1=neg_max[:, :, MROW:MROW + H], op0=ALU.mult, op1=ALU.subtract).then_inc(msplit, 1)

            def stack_k(j, i):
                dve.wait_ge(stage_in["k"], STAGED * (NC4 * j + i + 1))
                wait(dve, st_mm, H * (j - 1) + KC * (i + 1))
                dve.tensor_copy(k_st[0:MROW, i::NC4, :], stage[0:MROW, SLOT["k"]]).then_inc(stacked["k"], 1)

            def rotate(j, which, half):
                base = ROPE_OPS * j + 3 * half
                a, b = (z[:].rearrange("p (c s) -> p c s", c=2) for z in (q_bank if which == "q" else kv_bank))
                cos, sin = rope[:, 0], rope[:, 1]
                s = rope_step[which]
                if half == 0:
                    dve.wait_ge(qk_mm[which], 2 * (j + 1))
                    if which == "k":
                        wait(dve, lo_done["q"], 2 * j)
                        wait(dve, dmax_done, 2 * (j - 2))
                    else:
                        dve.wait_ge(lo_done["k"], 2 * (j + 1))
                dve.tensor_tensor(rt[:, 0], a, (cos, sin)[half], ALU.mult).then_inc(s, 1)
                dve.tensor_tensor(rt[:, 1], b, (sin, cos)[half], ALU.mult).then_inc(s, 1)
                dve.wait_ge(s, base + 2)
                dve.tensor_tensor(roped[:, 2 * half:2 * half + 2], rt[:, 0], rt[:, 1],
                                  (ALU.subtract, ALU.add)[half]).then_inc(s, 1)
                dve.wait_ge(s, base + 3)

            def rest(src, s, lead, count, done):
                dve.wait_ge(lead, count)
                tok = slice(s * P, (s + 1) * P)
                dve.tensor_tensor(t_lo[:, :, tok], src[s][:].rearrange("p (c t) -> p c t", c=KC),
                                  t_hi[:, :, tok].bitcast(F32), ALU.subtract).then_inc(done, 1)

            def xt_rest(j, s):
                rest(q_bank, s, xt_hi, 2 * j + s + 1, xt_lo)

            def ot_rest(j, s):
                rest(pv_bank, s, ot_hi, 2 * j + s + 1, ot_lo)

            def normalise(b, i):
                src = pv_bank[i % 2][:, 0:2 * GW].rearrange("p (q c e) -> p q c e", q=2, c=KC)
                dve.wait_ge(pv_mm, H * b + KC * (i + 1))
                wait(dve, onorm, NC4 * b + i)
                dve.reciprocal(o_rec[:], src[:, :, :, DK:VW]).then_inc(rec_done, 1)
                dve.wait_ge(rec_done, NC4 * b + i + 1)
                dve.tensor_tensor(o_n[:, :, :, i], src[:, :, :, 0:DK], o_rec[:].to_broadcast([P, 2, KC, DK]), ALU.mult).then_inc(onorm, 1)

            def quantise_win(b):
                dve.wait_ge(win_in, 16 * (b + 1))
                wait(dve, wq_round, 2 * b)
                link = chain(dve, wq_chain, WQ_OPS * b)
                link(dve.tensor_reduce(w_s[:, 0:1], w_raw[:], AX_X, ALU.max, apply_absolute_value=True))
                link(dve.tensor_scalar(w_s[:, 1:2], w_s[:, 0:1], QMIN, None, ALU.max))
                link(dve.reciprocal(w_s[:, 2:3], w_s[:, 1:2]))
                link(dve.tensor_scalar(w_s[:, 3:4], w_s[:, 2:3], 127.0, None, ALU.mult))
                link(dve.tensor_copy(win_amax[:, bass.ds(b, 1)], w_s[:, 1:2]))
                assert link.count[0] == WQ_OPS

            ln1_moments(0)
            dve.memset(neg_max[:], 0.0).then_inc(const_done, 1)
            dve.memset(magic_c[:], MAGIC).then_inc(const_done, 1)
            dve.wait_ge(ident_in, 16)
            dve.tensor_copy(ident_b[:], ident[:]).then_inc(const_done, 1)
            dve.wait_ge(const_done, CONSTS)

            def weight_lo(i, n):
                dve.wait_ge(w_hi_done, i + 1)
                dve.tensor_tensor(w_lo[n][:], weight_stage[n], w_hi[n][:].bitcast(F32), ALU.subtract).then_inc(w_lo_done, 1)

            xt_rest(0, 0)
            xt_rest(0, 1)
            for i, n in enumerate(("wk", "wq", "wv")):
                weight_lo(i, n)
            dve.wait_ge(w_lo_done, 1)
            dve.memset(v_sb[:, :, :, :, DK:VW], 1.0).then_inc(ones_done, 1)
            dve.wait_ge(c_in, 16 * TABLES)
            for which in ("k", "q"):
                rotate(0, which, 0)
                rotate(0, which, 1)
            weight_lo(3, "wo")
            ln1_moments(1)
            for i in range(NC4):
                stack_k(0, i)

            def step(b, par, has_c, has_o, has_proj, has_xt):
                between = {p: [] for p in range(H // 2)}
                if has_c:
                    between[0] += [lambda: largest(b - 2, 0), lambda: largest(b - 2, 1)]
                if has_proj:
                    between[1] += [lambda: rotate(b + 1, "k", 0)]
                    between[2] += [lambda: xt_rest(b + 1, 0), lambda: xt_rest(b + 1, 1)]
                    between[3] += [lambda: rotate(b + 1, "k", 1)]
                if has_o:
                    between[6] += [lambda: ot_rest(b - 1, 0), lambda: ot_rest(b - 1, 1)]
                for n in range(H):
                    row_maxima(b, n)
                    if n % 2:
                        for work in between[n // 2]:
                            work()
                split_max(b)
                if has_proj:
                    rotate(b + 1, "q", 0)
                    rotate(b + 1, "q", 1)
                    stack_k(b + 1, 0)
                quantise_win(b)
                normalise(b, 0)
                if has_xt:
                    ln1_moments(b + 2)
                if has_proj:
                    stack_k(b + 1, 1)
                if has_o:
                    residual(b - 1, 0)
                normalise(b, 1)
                if has_proj:
                    stack_k(b + 1, 2)
                normalise(b, 2)
                if has_o:
                    residual(b - 1, 1)
                    ln2_moments(b - 1)
                normalise(b, 3)
                if has_proj:
                    stack_k(b + 1, 3)

            steps(dve, step)
            largest(NB - 2, 0)
            largest(NB - 2, 1)
            ot_rest(NB - 1, 0)
            ot_rest(NB - 1, 1)
            residual(NB - 1, 0)
            residual(NB - 1, 1)
            ln2_moments(NB - 1)
            link = chain(dve, ln2_end, 0)
            link(dve.tensor_scalar(veps2[:], ln2_mv[:, :, 1], EPS, None, ALU.add))
            rsqrt_seed(dve, link, veps2[:], ln2_r[:])
            rsqrt(dve, link, veps2[:], ln2_r[:], nt_t2[:])
            link(dve.scalar_tensor_tensor(out=ln2_b[:], in0=ln2_mv[:, :, 0], scalar=-1.0,
                                          in1=ln2_r[:], op0=ALU.mult, op1=ALU.mult))
            largest(NB - 1, 0)
            largest(NB - 1, 1)
            dve.wait_ge(dmax_done, 2 * NB)
            link(dve.tensor_tensor(ymax[:], dmax[:], ln2_r[:], ALU.mult))
            dve.drain().then_inc(a_done, 1)
            dve.wait_ge(a_done, 4)

            dve.tensor_reduce(tiny[:, 0:1], ymax[:], AX_X, ALU.max).then_inc(bset, 1)
            dve.wait_ge(bset_pool, 1)
            link = chain(dve, bset, 1)
            link(dve.tensor_scalar(tiny[:, 2:3], tiny[:, 1:2], QMIN, None, ALU.max))
            link(dve.reciprocal(tiny[:, 3:4], tiny[:, 2:3]))
            link(dve.tensor_scalar(tiny[:, 4:5], tiny[:, 3:4], 32767.0, None, ALU.mult))
            link(dve.tensor_scalar(x_a[:], ln2_r[:], tiny[:, 4:5], None, ALU.mult))
            link(dve.tensor_scalar(x_b[:], ln2_b[:], tiny[:, 4:5], None, ALU.mult))
            link(dve.tensor_scalar(tiny[:, 6:7], tiny[:, 2:3], 1.0 / 32767.0, 1.0 / 127.0, ALU.mult, ALU.mult))
            dve.tensor_scalar(g_scale[:], win_amax[:], tiny[:, 6:7], None, ALU.mult).then_inc(bset, 1)

            def round_tile(n, par):
                for u in range(SUB):
                    dve.wait_ge(z_done, SUB * n + u + 1)
                    dve.tensor_scalar(xq[:, par, u], xq[:, par, u], MAGIC, MAGIC, ALU.add, ALU.subtract).then_inc(z_round, 1)

            def rest(n, par):
                for c in range(KC):
                    dve.wait_ge(qt_hi, KC * n + c + 1)
                    dve.tensor_tensor(qT_lo[:, par, c], bank[4 + c][:], qT_hi[:, par, c], ALU.subtract).then_inc(qt_lo, 1)

            def quantise_wout(j, par):
                link = chain(dve, wo_chain, WO_OPS * j)
                col = bass.ds(j, 1)
                s = wp_s[:, par]
                dve.wait_ge(wo_raw_in[par], 8 * j + (16 if par == 0 else 8))
                link(dve.tensor_reduce(s[:, 0:1], wo_raw[:, par], AX_X, ALU.max, apply_absolute_value=True))
                link(dve.tensor_scalar(s[:, 1:2], s[:, 0:1], QMIN, None, ALU.max))
                link(dve.reciprocal(s[:, 2:3], s[:, 1:2]))
                link(dve.tensor_scalar(s[:, 3:4], s[:, 2:3], 127.0, None, ALU.mult))
                link(dve.tensor_scalar(wout_amax[:, col], s[:, 1:2], 1.0 / 127.0, None, ALU.mult))
                link(dve.tensor_scalar(wout_pow[:, col].bitcast(I32), wout_amax[:, col].bitcast(I32), 0x7F800000, None, ALU.bitwise_and))
                link(dve.tensor_scalar(wo_raw[:, par], wo_raw[:, par], s[:, 3:4], MAGIC, ALU.mult, ALU.add))
                link(dve.tensor_scalar(wout_int[:, bass.ds(j, 1)].rearrange("p o d -> p (o d)"), wo_raw[:, par], MAGIC,
                                       wout_pow[:, col], ALU.subtract, ALU.mult))
                assert link.count[0] == WO_OPS

            def tile_b(n, par, spilt, more):
                for f in range(FC):
                    dve.wait_ge(gelu_done, FC * n + f + 1)
                    src = h_ring[:, f % 4] if spilt else h_kept[:, (n - SPILT) * FC + f]
                    dve.tensor_reduce(hmax[:, bass.ds(FC * n + f, 1)], src, AX_X, ALU.max,
                                      apply_absolute_value=True).then_inc(hmax_done, 1)
                    if f == 5 and more:
                        round_tile(n + 1, 1 - par)
                    if f == 7:
                        quantise_wout(2 * n, 0)
                    if f == 11 and more:
                        rest(n + 1, 1 - par)
                    if f == 14:
                        quantise_wout(2 * n + 1, 1)

            round_tile(0, 0)
            rest(0, 0)
            tile_b(0, 0, True, True)
            tile_b(1, 1, True, True)
            with dve.Fori(1, SPILT // 2) as i:
                tile_b(2 * i, 0, True, True)
                tile_b(2 * i + 1, 1, True, True)
            for n in range(SPILT, NT):
                tile_b(n, n % 2, False, n + 1 < NT)

            dve.wait_ge(hmax_done, FC * NT)
            dve.tensor_reduce(tiny[:, 0:1], hmax[:], AX_X, ALU.max).then_inc(cset, 1)
            dve.wait_ge(cset_pool, 1)
            link = chain(dve, cset, 1)
            link(dve.tensor_scalar(tiny[:, 2:3], tiny[:, 1:2], QMIN, None, ALU.max))
            link(dve.reciprocal(tiny[:, 3:4], tiny[:, 2:3]))
            link(dve.tensor_scalar(tiny[:, 5:6], tiny[:, 3:4], 32767.0, None, ALU.mult))
            link(dve.tensor_scalar(tiny[:, 6:7], tiny[:, 2:3], 2.0 / 32767.0, None, ALU.mult))
            link(dve.tensor_scalar(wout_man[:].bitcast(I32), wout_amax[:].bitcast(I32), 0x007FFFFF, 0x3F800000,
                                   ALU.bitwise_and, ALU.bitwise_or))
            link(dve.tensor_scalar(wout_man[:], wout_man[:], 0.5, None, ALU.mult))

            def integers(i, f):
                dve.wait_ge(hint_done, FC * i + f + 1)
                dve.tensor_scalar(h_int[:, f % 4], h_int[:, f % 4], MAGIC, wout_man[:, f:f + 1],
                                  ALU.subtract, ALU.mult).then_inc(g_done, 1)

            def result(i, par):
                dve.wait_ge(y_mm, FC * (i + 1))
                dve.wait_ge(xc_b, SUB * (i + 1))
                for u in range(SUB):
                    if u < 2:
                        wait(dve, y_out[u], 32 * i)
                    else:
                        dve.wait_ge(y_out[u % 2], 32 * i + 16)
                    dve.scalar_tensor_tensor(out=o_out[:, u % 2], in0=bank[4 * par + u][:], scalar=tiny[:, 6:7],
                                             in1=xq[:, par, u], op0=ALU.mult, op1=ALU.add).then_inc(y_done, 1)

            def tile_c(i, par, has_last):
                for f in range(FC):
                    integers(i, f)
                    dve.wait_ge(ghi_done, FC * i + f + 1)
                    dve.tensor_tensor(g_lo[:, f % 4], h_int[:, f % 4], g_hi[:, f % 4], ALU.subtract).then_inc(glo_done, 1)
                    if f == 4 and has_last:
                        result(i - 1, 1 - par)

            tile_c(0, 0, False)
            tile_c(1, 1, True)
            with dve.Fori(1, NT // 2) as i:
                tile_c(2 * i, 0, True)
                tile_c(2 * i + 1, 1, True)
            result(NT - 1, 1)

        @block.gpsimd
        def _(pool):
            def split_lo(which, j, half):
                c = slice(2 * half, 2 * half + 2)
                if half == 0:
                    pool.wait_ge(hi_done[which], j + 1)
                pool.tensor_tensor(part_lo[which][:, c], roped[:, c], part_hi[which][:, c].bitcast(F32), ALU.subtract).then_inc(lo_done[which], 1)

            def ctx_lo(j, half):
                c = slice(2 * half, 2 * half + 2)
                if half == 0:
                    pool.wait_ge(c_hi, j + 1)
                pool.tensor_tensor(cT_lo[:, c], ctx_raw[:, c], cT_hi[:, c].bitcast(F32), ALU.subtract).then_inc(c_lo, 1)

            def bias_x(j):
                pool.wait_ge(xres_in, 16 * (j + 1))
                for s in range(2):
                    pool.tensor_tensor(x_res[:, s], x_res[:, s], wo_b[:], ALU.add).then_inc(xres_b, 1)

            def ln1_scale(j):
                pool.wait_ge(ln1_moment, LN_ST * (j + 1))
                link = chain(pool, ln1_chain, LN_SC * j, separate=True)
                apart(pool)
                rsqrt(pool, link, veps[:], rstd[:], nt_t[:])
                link(pool.tensor_tensor(nmr[:], mv[:, 0, :, 0], rstd[:], ALU.mult))
                link(pool.tensor_scalar(nmr[:], nmr[:], -1.0, None, ALU.mult))
                assert link.count[0] == LN_SC

            def round_win(b):
                pool.wait_ge(wq_chain, WQ_OPS * (b + 1))
                wait(pool, wt_mm, b)
                apart(pool)
                pool.tensor_scalar(w_raw[:], w_raw[:], w_s[:, 3:4], MAGIC, ALU.mult, ALU.add).then_inc(wq_round, 1)
                pool.wait_ge(wq_round, 2 * b + 1)
                apart(pool)
                pool.tensor_scalar(w_q[:], w_raw[:], MAGIC, None, ALU.subtract).then_inc(wq_round, 1)

            def band(b, n):
                pool.wait_ge(exp_done, H * b + n + 1)
                apart(pool)
                lower, upper = probs[:, n % 4, 0, P:2 * P], probs[:, n % 4, 1, 0:P]
                pool.affine_select(out=lower, in_=lower, compare_op=ALU.is_ge, fill=0.0, base=0,
                                   pattern=[[-1, P]], channel_multiplier=1).then_inc(p_ready, 1)
                pool.affine_select(out=upper, in_=upper, compare_op=ALU.is_ge, fill=0.0, base=0,
                                   pattern=[[1, P]], channel_multiplier=-1).then_inc(p_ready, 1)

            ln1_scale(0)
            ctx_lo(0, 0)
            ctx_lo(0, 1)
            pool.wait_ge(c_in, 16 * TABLES)
            pool.wait_ge(c_lo, 2)
            pool.tensor_copy(k_st[MROW:P], sel[MROW:P].rearrange("p (h o) -> p h o", o=1).to_broadcast([P - MROW, H, S])).then_inc(sel_done, 1)
            pool.wait_ge(sel_done, 1)
            for which in ("k", "q"):
                split_lo(which, 0, 0)
                split_lo(which, 0, 1)
            ctx_lo(1, 0)
            ctx_lo(1, 1)

            def step(b, par, has_c, has_o, has_proj, has_xt):
                if has_proj:
                    ln1_scale(b + 1)
                if has_o:
                    bias_x(b - 1)
                if has_proj:
                    split_lo("k", b + 1, 0)
                    split_lo("k", b + 1, 1)
                for n in range(H):
                    band(b, n)
                    if n in (5, 6) and has_proj:
                        split_lo("q", b + 1, n - 5)
                    if n in (9, 11) and has_xt:
                        ctx_lo(b + 2, (n - 9) // 2)
                    if n == 13:
                        round_win(b)

            steps(pool, step)
            bias_x(NB - 1)
            pool.drain().then_inc(a_done, 1)
            pool.wait_ge(a_done, 4)

            pool.wait_ge(bset, 1)
            pool.partition_all_reduce(tiny[:, 1:2], tiny[:, 0:1], P, ABSMAX).then_inc(bset_pool, 1)
            pool.wait_ge(cset, 1)
            pool.partition_all_reduce(tiny[:, 1:2], tiny[:, 0:1], P, ABSMAX).then_inc(cset_pool, 1)
            pool.wait_ge(b_out_in, 16)

            def bias_tile(i, par):
                pool.wait_ge(xc_in[par], 8 * i + (16 if par == 0 else 8))
                for u in range(SUB):
                    pool.tensor_tensor(xq[:, par, u], xq[:, par, u], b_out[:], ALU.add).then_inc(xc_b, 1)

            with pool.Fori(0, NT // 2) as i:
                bias_tile(2 * i, 0)
                bias_tile(2 * i + 1, 1)


_WEIGHTS = {"wq": "L0_xattn_wq", "wk": "L0_xattn_wk", "wv": "L0_xattn_wv", "wo": "L0_xattn_wo_w"}


def kernel(**inputs):
    import concourse.bacc as _bacc
    from concourse.bass_utils import run_bass_kernel_spmd as _run

    a = {k: np.asarray(v) for k, v in inputs.items()}
    arrays = {"x": a["x"].reshape(TOK, D), "ctxT": a["ctx_1024"].reshape(TOK, D).T}
    for n, full in _WEIGHTS.items():
        arrays[n] = a[full].T
    arrays["wo_b"] = np.tile(a["L0_xattn_wo_b"], (P, 1))
    arrays["winT"] = a["L0_ffn_W_in"].T
    arrays["b_in"] = a["L0_ffn_b_in"].reshape(FC, P).T
    arrays["wout"] = a["L0_ffn_W_out"]
    arrays["b_out"] = np.tile(a["L0_ffn_b_out"], (P, 1))
    arrays.update(constants())
    arrays = {n: np.ascontiguousarray(v) for n, v in arrays.items()}

    nc = _bacc.Bacc("TRN2", target_bir_lowering=False, num_devices=1)
    t = {n: nc.dram_tensor("in_" + n, v.shape, mybir.dt.from_np(v.dtype), kind="ExternalInput").ap()
         for n, v in arrays.items()}
    t["out"] = nc.dram_tensor("out_0", (TOK, D), F32, kind="ExternalOutput").ap()
    build(nc, t)
    r = _run(nc, [{"in_" + n: v for n, v in arrays.items()}], core_ids=[0])
    return r.results[0]["out_0"].reshape(NB, S, D)
```
